# Optimizing a Trainium2 kernel written in Bass

```python
import numpy as np
import jax
import jax.numpy as jnp

def _softmax(x, axis=-1):
    return jax.nn.softmax(x, axis=axis)

def _gelu(x):
    return jax.nn.gelu(x, approximate=True)

def _silu(x):
    return jax.nn.silu(x)

def _sigmoid(x):
    return jax.nn.sigmoid(x)

def _layernorm(x, axis=-1, eps=1e-05):
    m = jnp.mean(x, axis=axis, keepdims=True)
    v = jnp.var(x, axis=axis, keepdims=True)
    return (x - m) / jnp.sqrt(v + eps)

def _scatter_add(tgt, idx, src, axis=0):
    return tgt.at[idx].add(src)

def _segment_sum(src, seg, n):
    return jax.ops.segment_sum(src, seg, n)
kernel_name = 'mk_cond_seq_d2_seqx_r4_5146c9'

def setup_inputs(seed: int=0):
    np.random.seed(seed)
    _w = jnp.asarray

    def _rec_inputs():
        import jax
        import jax.numpy as jnp
        _rk = jax.random.key(seed)
        x = -0.0002928 + 1 * jax.random.normal(jax.random.fold_in(_rk, 1), (2, 1024, 256), jnp.float32)
        _lenS = 1024 - jax.random.randint(jax.random.fold_in(_rk, 7), (2,), 0, max(1, 1024 // 4) + 1, jnp.int32)
        _lenS2 = 1024 - jax.random.randint(jax.random.fold_in(_rk, 8), (2,), 0, max(1, 1024 // 4) + 1, jnp.int32)
        cond_1024 = 0.0061147 + 1.02565 * jax.random.normal(jax.random.fold_in(_rk, 11), (2, 256), jnp.float32)
        _validS = jnp.arange(1024)[None, :] < _lenS[:, None]
        _validS2 = jnp.arange(1024)[None, :] < _lenS2[:, None]
        _causal = jnp.tril(jnp.ones((1024, 1024), dtype=bool))
        mask_BxS_bk0 = jnp.logical_not(jnp.broadcast_to(_validS[:, :], (2, 1024)))
        return (x, cond_1024, mask_BxS_bk0)
    x, cond_1024, mask_BxS_bk0 = _rec_inputs()

    def _L0_cond_setup():
        import jax, jax.numpy as jnp
        import numpy as np
        B, N, C = (4, 256, 256)
        H = 16
        D = C // H
        FF = 4 * C
        EPS = 1e-05

        def _layernorm(x):
            mu = jnp.mean(x, axis=-1, keepdims=True)
            var = jnp.mean(jnp.square(x - mu), axis=-1, keepdims=True)
            return (x - mu) * jax.lax.rsqrt(var + EPS)

        def _modulate(x, shift, scale):
            return x * (1.0 + scale[:, None, :]) + shift[:, None, :]

        def _attention(x, node_mask, qkv_w, proj_w, proj_b):
            b, n, c = x.shape
            qkv = (x @ qkv_w).reshape(b, n, 3, H, D)
            q, k, v = jnp.moveaxis(qkv, 2, 0)
            q = q.transpose(0, 2, 1, 3)
            k = k.transpose(0, 2, 1, 3)
            v = v.transpose(0, 2, 1, 3)
            scale = D ** (-0.5)
            scores = jnp.einsum('bhnd,bhmd->bhnm', q, k) * scale
            mask = node_mask[:, None, None, :]
            scores = jnp.where(mask, scores, -jnp.inf)
            attn = jax.nn.softmax(scores, axis=-1)
            out = jnp.einsum('bhnm,bhmd->bhnd', attn, v)
            out = out.transpose(0, 2, 1, 3).reshape(b, n, c)
            return out @ proj_w + proj_b

        def _mlp(x, fc1_w, fc1_b, fc2_w, fc2_b):
            h = jax.nn.gelu(x @ fc1_w + fc1_b, approximate=False)
            return h @ fc2_w + fc2_b
        key = jax.random.key(seed)
        ks = jax.random.split(key, 16)
        s = 0.02
        return {'x': jax.random.normal(ks[0], (B, N, C), jnp.float32), 'c': jax.random.normal(ks[1], (B, C), jnp.float32), 'node_mask': jax.random.randint(ks[2], (B, N), 0, 2) > 0, 'qkv_w': jax.random.normal(ks[3], (C, 3 * C), jnp.float32) * s, 'proj_w': jax.random.normal(ks[4], (C, C), jnp.float32) * s, 'proj_b': jnp.zeros((C,), jnp.float32), 'fc1_w': jax.random.normal(ks[5], (C, FF), jnp.float32) * s, 'fc1_b': jnp.zeros((FF,), jnp.float32), 'fc2_w': jax.random.normal(ks[6], (FF, C), jnp.float32) * s, 'fc2_b': jnp.zeros((C,), jnp.float32), 'ada1_w': jax.random.normal(ks[7], (C, C), jnp.float32) * s, 'ada1_b': jnp.zeros((C,), jnp.float32), 'ada2_w': jax.random.normal(ks[8], (C, 6 * C), jnp.float32) * s, 'ada2_b': jnp.zeros((6 * C,), jnp.float32)}
    _L0_cond_all = _L0_cond_setup()
    _L0_cond_in = {k: v for k, v in _L0_cond_all.items() if k in ('qkv_w', 'proj_w', 'proj_b', 'fc1_w', 'fc1_b', 'fc2_w', 'fc2_b', 'ada1_w', 'ada1_b', 'ada2_w', 'ada2_b')}
    del _L0_cond_all

    def _L1_cond_setup():
        import jax, jax.numpy as jnp
        import numpy as np
        DIM = 256
        FF_MULT = 2
        EPS = 1e-06

        def _ln(x):
            mu = jnp.mean(x, axis=-1, keepdims=True)
            var = jnp.mean(jnp.square(x - mu), axis=-1, keepdims=True)
            return (x - mu) * jax.lax.rsqrt(var + EPS)
        key = jax.random.key(seed)
        ks = jax.random.split(key, 12)
        b, n, d = (4, 512, DIM)
        h = FF_MULT * d
        s = lambda fan_in: 1.0 / np.sqrt(fan_in)
        return {'x': jax.random.normal(ks[0], (b, n, d), jnp.float32), 't': jax.random.normal(ks[1], (b, d), jnp.float32), 'ada_w': jax.random.normal(ks[2], (d, 6 * d), jnp.float32) * s(d), 'ada_b': jnp.zeros((6 * d,), jnp.float32), 'ssm_w1': jax.random.normal(ks[3], (d, d), jnp.float32) * s(d), 'ssm_b1': jnp.zeros((d,), jnp.float32), 'ssm_w2': jax.random.normal(ks[4], (d, d), jnp.float32) * s(d), 'ssm_b2': jnp.zeros((d,), jnp.float32), 'ff_w1': jax.random.normal(ks[5], (d, h), jnp.float32) * s(d), 'ff_b1': jnp.zeros((h,), jnp.float32), 'ff_w2': jax.random.normal(ks[6], (h, d), jnp.float32) * s(h), 'ff_b2': jnp.zeros((d,), jnp.float32)}
    _L1_cond_all = _L1_cond_setup()
    _L1_cond_in = {k: v for k, v in _L1_cond_all.items() if k in ('ada_w', 'ada_b', 'ssm_w1', 'ssm_b1', 'ssm_w2', 'ssm_b2', 'ff_w1', 'ff_b1', 'ff_w2', 'ff_b2')}
    del _L1_cond_all
    return {'x': x, 'cond_1024': cond_1024, 'mask_BxS_bk0': mask_BxS_bk0, 'L0_cond_qkv_w': _L0_cond_in['qkv_w'], 'L0_cond_proj_w': _L0_cond_in['proj_w'], 'L0_cond_proj_b': _L0_cond_in['proj_b'], 'L0_cond_fc1_w': _L0_cond_in['fc1_w'], 'L0_cond_fc1_b': _L0_cond_in['fc1_b'], 'L0_cond_fc2_w': _L0_cond_in['fc2_w'], 'L0_cond_fc2_b': _L0_cond_in['fc2_b'], 'L0_cond_ada1_w': _L0_cond_in['ada1_w'], 'L0_cond_ada1_b': _L0_cond_in['ada1_b'], 'L0_cond_ada2_w': _L0_cond_in['ada2_w'], 'L0_cond_ada2_b': _L0_cond_in['ada2_b'], 'L1_cond_ada_w': _L1_cond_in['ada_w'], 'L1_cond_ada_b': _L1_cond_in['ada_b'], 'L1_cond_ssm_w1': _L1_cond_in['ssm_w1'], 'L1_cond_ssm_b1': _L1_cond_in['ssm_b1'], 'L1_cond_ssm_w2': _L1_cond_in['ssm_w2'], 'L1_cond_ssm_b2': _L1_cond_in['ssm_b2'], 'L1_cond_ff_w1': _L1_cond_in['ff_w1'], 'L1_cond_ff_b1': _L1_cond_in['ff_b1'], 'L1_cond_ff_w2': _L1_cond_in['ff_w2'], 'L1_cond_ff_b2': _L1_cond_in['ff_b2']}

def reference(x, cond_1024, mask_BxS_bk0, L0_cond_qkv_w, L0_cond_proj_w, L0_cond_proj_b, L0_cond_fc1_w, L0_cond_fc1_b, L0_cond_fc2_w, L0_cond_fc2_b, L0_cond_ada1_w, L0_cond_ada1_b, L0_cond_ada2_w, L0_cond_ada2_b, L1_cond_ada_w, L1_cond_ada_b, L1_cond_ssm_w1, L1_cond_ssm_b1, L1_cond_ssm_w2, L1_cond_ssm_b2, L1_cond_ff_w1, L1_cond_ff_b1, L1_cond_ff_w2, L1_cond_ff_b2):
    import jax
    import jax.numpy as jnp

    def _L0_cond_ref(x, c, node_mask, qkv_w, proj_w, proj_b, fc1_w, fc1_b, fc2_w, fc2_b, ada1_w, ada1_b, ada2_w, ada2_b):
        import jax, jax.numpy as jnp
        import numpy as np
        B, N, C = (4, 256, 256)
        H = 16
        D = C // H
        FF = 4 * C
        EPS = 1e-05

        def _layernorm(x):
            mu = jnp.mean(x, axis=-1, keepdims=True)
            var = jnp.mean(jnp.square(x - mu), axis=-1, keepdims=True)
            return (x - mu) * jax.lax.rsqrt(var + EPS)

        def _modulate(x, shift, scale):
            return x * (1.0 + scale[:, None, :]) + shift[:, None, :]

        def _attention(x, node_mask, qkv_w, proj_w, proj_b):
            b, n, c = x.shape
            qkv = (x @ qkv_w).reshape(b, n, 3, H, D)
            q, k, v = jnp.moveaxis(qkv, 2, 0)
            q = q.transpose(0, 2, 1, 3)
            k = k.transpose(0, 2, 1, 3)
            v = v.transpose(0, 2, 1, 3)
            scale = D ** (-0.5)
            scores = jnp.einsum('bhnd,bhmd->bhnm', q, k) * scale
            mask = node_mask[:, None, None, :]
            scores = jnp.where(mask, scores, -jnp.inf)
            attn = jax.nn.softmax(scores, axis=-1)
            out = jnp.einsum('bhnm,bhmd->bhnd', attn, v)
            out = out.transpose(0, 2, 1, 3).reshape(b, n, c)
            return out @ proj_w + proj_b

        def _mlp(x, fc1_w, fc1_b, fc2_w, fc2_b):
            h = jax.nn.gelu(x @ fc1_w + fc1_b, approximate=False)
            return h @ fc2_w + fc2_b
        ada = jax.nn.silu(c @ ada1_w + ada1_b) @ ada2_w + ada2_b
        shift_msa, scale_msa, gate_msa, shift_mlp, scale_mlp, gate_mlp = jnp.split(ada, 6, axis=1)
        attn_out = _attention(x, node_mask, qkv_w, proj_w, proj_b)
        x = x + gate_msa[:, None, :] * _modulate(_layernorm(attn_out), shift_msa, scale_msa)
        mlp_out = _mlp(x, fc1_w, fc1_b, fc2_w, fc2_b)
        x = x + gate_mlp[:, None, :] * _modulate(_layernorm(mlp_out), shift_mlp, scale_mlp)
        return x

    def _L1_cond_ref(x, t, ada_w, ada_b, ssm_w1, ssm_b1, ssm_w2, ssm_b2, ff_w1, ff_b1, ff_w2, ff_b2):
        import jax, jax.numpy as jnp
        import numpy as np
        DIM = 256
        FF_MULT = 2
        EPS = 1e-06

        def _ln(x):
            mu = jnp.mean(x, axis=-1, keepdims=True)
            var = jnp.mean(jnp.square(x - mu), axis=-1, keepdims=True)
            return (x - mu) * jax.lax.rsqrt(var + EPS)
        emb = jnp.dot(jax.nn.silu(t), ada_w) + ada_b
        shift_msa, scale_msa, gate_msa, shift_mlp, scale_mlp, gate_mlp = jnp.split(emb, 6, axis=-1)
        norm = _ln(x) * (1.0 + scale_msa[:, None]) + shift_msa[:, None]
        h = jax.nn.gelu(jnp.dot(norm, ssm_w1) + ssm_b1, approximate=False)
        ssm_out = jnp.dot(h, ssm_w2) + ssm_b2
        x = x + gate_msa[:, None] * ssm_out
        norm2 = _ln(x) * (1.0 + scale_mlp[:, None]) + shift_mlp[:, None]
        hf = jax.nn.gelu(jnp.dot(norm2, ff_w1) + ff_b1, approximate=True)
        ff_out = jnp.dot(hf, ff_w2) + ff_b2
        x = x + gate_mlp[:, None] * ff_out
        return x
    x = _L0_cond_ref(x, cond_1024, mask_BxS_bk0, L0_cond_qkv_w, L0_cond_proj_w, L0_cond_proj_b, L0_cond_fc1_w, L0_cond_fc1_b, L0_cond_fc2_w, L0_cond_fc2_b, L0_cond_ada1_w, L0_cond_ada1_b, L0_cond_ada2_w, L0_cond_ada2_b)
    x = _L1_cond_ref(x, cond_1024, L1_cond_ada_w, L1_cond_ada_b, L1_cond_ssm_w1, L1_cond_ssm_b1, L1_cond_ssm_w2, L1_cond_ssm_b2, L1_cond_ff_w1, L1_cond_ff_b1, L1_cond_ff_w2, L1_cond_ff_b2)
    return x

_drawn_inputs = setup_inputs


def setup_inputs(seed=0):
    import zlib

    import numpy as np

    out = dict(_drawn_inputs(seed))
    spreads = {'L0_cond_proj_b': (0.0, 0.1),
     'L0_cond_fc1_b': (0.0, 0.298),
     'L0_cond_fc2_b': (0.0, 0.1),
     'L0_cond_ada1_b': (0.0, 0.333),
     'L0_cond_ada2_b': (0.0, 0.1),
     'L1_cond_ada_b': (0.0, 0.1),
     'L1_cond_ssm_b1': (0.0, 0.1),
     'L1_cond_ssm_b2': (0.0, 0.1),
     'L1_cond_ff_b1': (0.0, 0.274),
     'L1_cond_ff_b2': (0.0, 0.1)}
    factors = {}
    for name, (base, spread) in spreads.items():
        noise = np.random.default_rng([zlib.crc32(name.encode()), seed]).standard_normal(out[name].shape)
        drawn = base * np.exp(spread * noise) if base else spread * noise
        out[name] = jnp.asarray(drawn.astype(out[name].dtype))
    for name, factor in factors.items():
        out[name] = (out[name] * factor).astype(out[name].dtype)
    return out
```

```python
from contextlib import ExitStack

import concourse.bass as bass
from concourse import mybir

F32 = mybir.dt.float32
F32R = mybir.dt.float32r
U8 = mybir.dt.uint8
I32 = mybir.dt.int32
ALU = mybir.AluOpType
ACT = mybir.ActivationFunctionType
AX = mybir.AxisListType

B, N, C = 2, 1024, 256
P = 128
H, D = 16, 16
KC = C // P
CH = 512
NCH = N // CH
T = CH // P
HG = 4
NG = H // HG
UNITS = NCH * NG
VW = D + 1
FF0, FF1 = 4 * C, 2 * C
MASKED = -1e30
SCALE = D ** -0.5
EPS0, EPS1 = 1e-5, 1e-6
QSLOTS = 3
HSLOTS = 3

ROW_A, ROW_B, ROW_C = 0, 16, 32
ROW_MASK = 64
ROW_MAX = 96
ROWS_S1, ROWS_S2 = 96, 98

BANK_FEAT, BANK_TOK, BANK_PV, BANK_T = 0, 2, 6, 7

H1, G1, _, H2, G2, _, SH_S, SC_S, GS, SH_F, SC_F, GF, GSB, GFB = range(14)


class Path:

    def __init__(self, name, keys):
        self.name, self.keys = name, keys
        self.kt = keys // P
        self.block = min(CH, keys)
        self.blocks = keys // self.block
        self.n1 = HG * T * keys // CH
        self.n2 = 2 * self.kt
        self.heads = H if keys * H <= 4096 else HG

    def order(self):
        if self.kt == 2:
            return self.skewed()
        steps = [("k", n) for n in range(KC * self.blocks)] + [("v", n) for n in range(self.kt)]
        for u in range(UNITS):
            steps += [("ka", u), ("qa", u)] + [("s1", u, n) for n in range(self.n1)]
            steps += [("mneg", u), ("mT", u)]
            for kt in range(self.kt):
                steps += [("s2", u, kt, 0), ("s2", u, kt, 1)] + [("pv", u, kt - 1)] * (kt > 0)
            steps += [("pv", u, self.kt - 1), ("o", u), ("oT", u)]
            steps += [("attnT", u // NG)] * (u % NG == NG - 1)
        return steps

    def skewed(self):
        steps = [("k", n) for n in range(KC * self.blocks)] + [("v", n) for n in range(self.kt)]
        steps += [("ka", 0)] + [("qa", u) for u in range(QSLOTS)]
        tiles = [(u, n) for u in range(UNITS) for n in range(self.n1)]
        after = None

        def s1():
            nonlocal after
            u, n = tiles.pop(0)
            out = [("s1", u, n)]
            if after is not None and n == 1:
                out.append(("mT", after))
                after = None
            if n == self.n1 - 1:
                out.append(("mneg", u))
                after = u
            return out

        for _ in range(3 * self.n1 // 2):
            steps += s1()
        for u in range(UNITS):
            for i in range(self.n2):
                steps.append(("s2", u, i // 2, i % 2))
                for _ in range(self.n1 // self.n2):
                    steps += s1() if tiles else []
                if not tiles and after is not None:
                    steps.append(("mT", after))
                    after = None
                if i == 1 and u > 0:
                    steps += [("pv", u - 1, 1), ("o", u - 1)]
                if i == 3:
                    steps.append(("pv", u, 0))
                    if u > 0:
                        steps.append(("oT", u - 1))
                        steps += [("attnT", (u - 1) // NG)] * ((u - 1) % NG == NG - 1)
            if u + QSLOTS < UNITS:
                steps.append(("qa", u + QSLOTS))
        u = UNITS - 1
        return steps + [("pv", u, 1), ("o", u), ("oT", u), ("attnT", u // NG)]


FAST, FULL = Path("fast", 256), Path("full", N)

MLP_ORDER = [("proj", 0), ("proj", 1), ("T1", 0), ("fc", 0), ("T1", 1), ("fc", 1), ("T2", 0),
             ("ssm", 0), ("T2", 1), ("ssm", 1), ("T3", 0), ("ff", 0), ("T3", 1), ("ff", 1)]
HIDDEN = {"fc": FF0 // P, "ssm": C // P, "ff": FF1 // P}


def numbered(kinds, each):
    at, n = {}, 0
    for step in kinds:
        at[step] = n
        n += each(step)
    return at, n


T_AT, T_N = numbered([("x", 0), ("x", 1), ("o", 0), ("o", 1)] + [s for s in MLP_ORDER if s[0][0] == "T"],
                     lambda s: T // 2)
MLPS = [s for s in MLP_ORDER if s[0] in HIDDEN]
H_AT, H_N = numbered(MLPS, lambda s: HIDDEN[s[0]])
TOK_AT, TOK_N = numbered([s for s in MLP_ORDER if s[0][0] != "T"], lambda s: T)
LN_AT, LN_N = numbered([("proj", 0), ("proj", 1), ("fc", 0), ("T2", 0), ("fc", 1), ("T2", 1), ("T3", 0), ("T3", 1)],
                       lambda s: T // 2)
Q_N = KC * NCH


def t_bank(n):
    return BANK_T if T_AT["o", 0] <= n < T_AT["T1", 0] else BANK_PV + n % 2


def t_before(n):
    return max([m for m in range(n) if t_bank(m) == t_bank(n)], default=-1)


def build(nc, x, cond, mask, qkv_w, proj_w, proj_b, fc1_w, fc1_b, fc2_w, fc2_b, ada1_w, ada1_b, ada2_w, ada2_b,
          adb_w, adb_b, ssm_w1, ssm_b1, ssm_w2, ssm_b2, ff_w1, ff_b1, ff_w2, ff_b2, out):
    ctx = ExitStack()
    with ctx:
        ctx.enter_context(nc.allow_non_contiguous_dma(reason="small vectors spread over partitions"))

        def sb(name, shape, dt=F32):
            return ctx.enter_context(nc.sbuf_tensor(name, shape, dt))

        def sem(name):
            return ctx.enter_context(nc.semaphore(name))

        q_dram = nc.dram_tensor("q_dram", [2, C, N], F32, kind="Internal").ap()
        k_dram = nc.dram_tensor("k_dram", [2, C, N], F32, kind="Internal").ap()
        mod_dram = nc.dram_tensor("mod_dram", [B, 14, C], F32, kind="Internal").ap()
        neg_dram = nc.dram_tensor("neg_dram", [B, N], F32, kind="Internal").ap()

        weights = {}
        for name, rows, cols in (("qkv", C, 3 * C), ("proj", C, C), ("fc1", C, FF0), ("fc2", FF0, C),
                                 ("ssm1", C, C), ("ssm2", C, C), ("ff1", C, FF1), ("ff2", FF1, C)):
            weights[name] = [sb(f"{name}_{part}", [P, rows // P, cols], F32R) for part in ("hi", "lo")]
        x_tok = sb("x_tok", [P, NCH * T, C])
        actT = {s: [sb(f"act{s}_{part}", [P, KC, CH], F32R) for part in ("hi", "lo")] for s in "ABC"}
        qa = sb("qa", [ROWS_S2, QSLOTS, HG, CH], F32R)
        ka = sb("ka", [ROWS_S2, H * FAST.keys], F32R)
        v_sb = sb("v_sb", [P, N // P, H, VW])
        probs = sb("probs", [P, 2, HG, CH])
        o_sb = sb("o_sb", [P, 2, CH])
        o_tok = sb("o_tok", [P, T, C])
        hid = sb("hid", [P, HSLOTS, 2, CH], F32R)
        stage = sb("stage", [P, 6 * C])
        vec = sb("vec", [P, 10, C])
        cols = sb("cols", [P, KC, 4, B])
        ident = sb("ident", [P, P])
        mpart = sb("mpart", [P, 2, HG, T, 2])
        mmax = sb("mmax", [P, 2, HG * T])
        mhl = sb("mhl", [P, 2, 2 * HG * T], F32R)
        m_rows = sb("m_rows", [2 * HG * T, 2, P], F32R)
        rden = sb("rden", [P, T, HG])
        mask_rows = sb("mask_rows", [B * N // P, P], U8)
        mask_neg = sb("mask_neg", [B * N // P, P], F32R)
        mask_col = sb("mask_col", [P, B * N // P])
        flags = sb("flags", [1, 2 * B], I32)
        condT = sb("condT", [P, KC, B])
        silu0 = sb("silu0", [P, KC, B])
        silu1 = sb("silu1", [P, KC, B])
        ada1b = sb("ada1b", [P, KC])
        fc1b = sb("fc1b", [P, FF0 // P])
        upb = sb("upb", [P, (C + FF1) // P])
        upb_mod = sb("upb_mod", [P, (C + FF1) // P, B])
        stats = sb("stats", [P, 2, 6])
        mv = sb("mv", [P, 4, 2, 2])
        veps = sb("veps", [P, 4, 2])
        rstd = sb("rstd", [P, 4, 2])
        mhalf = sb("mhalf", [P, 2])
        eps0 = sb("eps0", [P, 2])
        eps1 = sb("eps1", [P, 2])
        scratch = probs[:, :, :, :].rearrange("p a h n -> p (a h n)")
        gelu_out = scratch[:, 0:2 * CH].rearrange("p (s n) -> p s n", s=2)
        a_tok = [scratch[:, 2 * CH + c * T * C:2 * CH + (c + 1) * T * C].rearrange("p (t c) -> p t c", t=T) for c in range(NCH)]
        qkv_raw = v_sb[:, :, :, :].rearrange("p a h n -> p (a h n)")[:, 0:6 * C].rearrange("p (k n) -> p k n", k=KC)
        ada_raw = scratch[:, 0:12 * C].rearrange("p (k n) -> p k n", k=KC)
        mask_f = scratch[0:B * N // P, 12 * C:12 * C + P]
        mask_line = scratch[0:1, 13 * C:15 * C].bitcast(U8).rearrange("o (b n) -> o b n", b=B)
        ada1_raw = o_tok[:, :, :].rearrange("p t c -> p (t c)")[:, 0:2 * C].rearrange("p (k n) -> p k n", k=KC)
        ada_row = vec[0:B, 0:8, :]
        bias_row = stage[0:B, :].rearrange("b (r c) -> b r c", c=C)
        down_b_row = o_sb[0:B, :, 0:C]

        ps = ctx.enter_context(nc.psum_tensor("ps", [P, 8, 512], F32))

        s_x = [sem(f"x_loaded{c}") for c in range(NCH)]
        s_mask, s_qkv_raw, s_small, s_cond = sem("mask_loaded"), sem("qkv_loaded"), sem("small_loaded"), sem("cond_loaded")
        s_ada_raw = [sem(f"ada_loaded{n}") for n in range(2)]
        s_bias_row = [sem(f"bias_row_loaded{n}") for n in range(2)]
        s_stage, s_staged = sem("stage_loaded"), sem("stage_used")
        s_ident, s_const, s_dset = sem("ident_made"), sem("consts_made"), sem("dve_setup")
        s_maskT, s_flags = sem("mask_transposed"), sem("flags_made")
        s_qkv_hi, s_qkv_lo = sem("qkv_hi_made"), sem("qkv_lo_made")
        s_ada_mm, s_silu, s_ada_row, s_mod_out = sem("ada_mm"), sem("silu_made"), sem("ada_rows_made"), sem("mod_stored")
        s_vec, s_cols, s_upb = sem("vec_loaded"), sem("cols_loaded"), sem("up_bias_made")
        s_neg_out, s_split, s_poolw = sem("neg_stored"), sem("weights_split"), sem("pool_weights")
        s_alone = sem("waits_alone")
        s_t_mm, s_t_hi, s_t_lo = sem("transposed"), sem("transposed_hi"), sem("transposed_lo")
        s_q_mm, s_q_hi, s_q_lo = sem("q_mm"), sem("q_hi"), sem("q_lo")
        s_q_out = [sem(f"q_stored{c}") for c in range(NCH)]
        s_tok_mm, s_tok_free = sem("tok_mm"), sem("tok_evacuated")
        s_up_mm, s_gelu, s_h_hi, s_h_lo, s_h_used = sem("up_mm"), sem("gelu_made"), sem("h_hi"), sem("h_lo"), sem("h_used")
        s_bn, s_aggr, s_eps, s_rstd = sem("bn_stats"), sem("bn_aggr"), sem("eps_added"), sem("rstd_made")
        s_cen, s_norm = sem("centred"), sem("normalised")
        s_res = sem("residual_shifted")
        s_wmod = sem("weights_modulated")
        s_out = [sem(f"out_stored{c}") for c in range(NCH)]

        class PathSems:
            def __init__(self, p):
                self.k_mm, self.k_hi, self.k_lo = [sem(f"{p.name}_k_{w}") for w in ("mm", "hi", "lo")]
                self.k_out, self.ka = sem(f"{p.name}_k_stored"), sem(f"{p.name}_keys_packed")
                self.v_mm, self.v = sem(f"{p.name}_v_mm"), sem(f"{p.name}_v_made")
                self.qa = [sem(f"{p.name}_queries_packed{n}") for n in range(QSLOTS)]
                self.m = [sem(f"{p.name}_max_packed{n}") for n in range(QSLOTS)]
                self.s1, self.max = sem(f"{p.name}_s1_mm"), sem(f"{p.name}_max")
                self.fold, self.neg, self.mT, self.mT_sb = [sem(f"{p.name}_m_{w}") for w in ("fold", "neg", "T", "T_copied")]
                self.s2, self.exp, self.pv = sem(f"{p.name}_s2_mm"), sem(f"{p.name}_exp"), sem(f"{p.name}_pv")
                self.o_sb, self.oT, self.rden, self.o = [sem(f"{p.name}_o_{w}") for w in ("copied", "T", "rden", "made")]

        sems = {p.name: PathSems(p) for p in (FAST, FULL)}
        block = ctx.enter_context(nc.Block())

        def slot_uses(u):
            return u // QSLOTS + 1

        def slot_total(u):
            return len([w for w in range(UNITS) if w % QSLOTS == u % QSLOTS])

        def x_tile(act, part, n0, n):
            c, at = n0 // CH, n0 % CH
            return [actT["AB"[c]][part][:, k, at:at + n] for k in range(KC)]

        def alone(e):
            e.sem_inc(s_alone, 1)

        def wait_before(e, b, semaphore, each):
            assert B == 2
            with e.If(b != 0):
                e.wait_ge(semaphore, each)
                e.nop()

        def batches(e, body):
            e.wait_ge(s_flags, 2)
            full0 = e.value_load(flags[0:1, 0:1], min_val=0, max_val=1)
            fast0 = e.value_load(flags[0:1, B:B + 1], min_val=0, max_val=1)
            with e.Fori(0, B) as b:
                body(b, {"full": b * full0, "fast": b * fast0})

        def by_path(e, b, seen, run):
            full = e.value_load(flags[0:1, bass.ds(b, 1)], min_val=0, max_val=1)
            with e.If(full != 0):
                run(FULL, sems["full"], seen["full"])
            with e.Else():
                run(FAST, sems["fast"], seen["fast"])

        @block.sync
        def _(sp):
            sp.dma_start(mask_rows[:, :], mask.rearrange("b (t p) -> (b t) p", p=P)).then_inc(s_mask, 16)
            sp.dma_start(mask_line, mask.rearrange("(o b) n -> o b n", o=1)).then_inc(s_mask, 16)
            for bb in range(B):
                sp.dma_start(condT[:, :, bb], cond[bb, :].rearrange("(k p) -> p k", p=P)).then_inc(s_cond, 16)
            sp.dma_start(ada1b[:, :], ada1_b.rearrange("(k p) -> p k", p=P)).then_inc(s_cond, 16)
            sp.dma_start(ada1_raw, ada1_w.rearrange("(k p) n -> p k n", p=P)).then_inc(s_cond, 16)
            sp.dma_start(qkv_raw, qkv_w.rearrange("(k p) n -> p k n", p=P)).then_inc(s_qkv_raw, 16)
            sp.dma_start(ada_raw, ada2_w.rearrange("(k p) n -> p k n", p=P)).then_inc(s_ada_raw[0], 16)
            sp.dma_start(bias_row, ada2_b.rearrange("(o r c) -> o r c", o=1, c=C).broadcast_to([B, 6, C]))\
                .then_inc(s_bias_row[0], 16)
            for r, b_dram in enumerate((ssm_b2, ff_b2)):
                sp.dma_start(down_b_row[:, r, :], b_dram.rearrange("(o c) -> o c", o=1).broadcast_to([B, C]))\
                    .then_inc(s_small, 16)
            sp.dma_start(fc1b[:, :], fc1_b.rearrange("(k p) -> p k", p=P)).then_inc(s_small, 16)
            sp.dma_start(upb[:, 0:C // P], ssm_b1.rearrange("(k p) -> p k", p=P)).then_inc(s_small, 16)
            sp.dma_start(upb[:, C // P:], ff_b1.rearrange("(k p) -> p k", p=P)).then_inc(s_small, 16)
            for r, b_dram in enumerate((proj_b, fc2_b)):
                sp.dma_start(vec[:, 8 + r, :], b_dram.rearrange("(o c) -> o c", o=1).broadcast_to([P, C]))\
                    .then_inc(s_small, 16)
            sp.wait_ge(s_dset, 2)
            sp.dma_start(neg_dram.rearrange("b (t p) -> (b t) p", p=P), mask_neg[:, :].bitcast(F32)).then_inc(s_neg_out, 16)
            sp.wait_ge(s_neg_out, 16)
            sp.wait_ge(s_ada_mm, 2)
            sp.dma_start(ada_raw, adb_w.rearrange("(k p) n -> p k n", p=P)).then_inc(s_ada_raw[1], 16)
            sp.wait_ge(s_ada_row, 5)
            sp.dma_start(bias_row, adb_b.rearrange("(o r c) -> o r c", o=1, c=C).broadcast_to([B, 6, C]))\
                .then_inc(s_bias_row[1], 16)
            sp.dma_start(mod_dram[:, 0:6, :], ada_row[:, 0:6, :]).then_inc(s_mod_out, 16)
            sp.wait_ge(s_ada_row, 10)
            sp.dma_start(mod_dram[:, 6:14, :], ada_row[:, 0:8, :]).then_inc(s_mod_out, 16)
            sp.dma_start(stage[:, 0:2 * C].rearrange("p (k n) -> p k n", k=KC),
                         ssm_w1.rearrange("(k p) n -> p k n", p=P)).then_inc(s_cols, 16)
            sp.dma_start(stage[:, 2 * C:6 * C].rearrange("p (k n) -> p k n", k=KC),
                         ff_w1.rearrange("(k p) n -> p k n", p=P)).then_inc(s_cols, 16)
            sp.wait_ge(s_mod_out, 32)
            for r, row in enumerate((SH_S, SC_S, SH_F, SC_F)):
                for bb in range(B):
                    sp.dma_start(cols[:, :, r, bb], mod_dram[bb, row, :].rearrange("(k p) -> p k", p=P)).then_inc(s_cols, 16)

            def body(b, seen):
                for c in range(NCH):
                    wait_before(sp, b, s_tok_free, TOK_N // 2)
                    sp.dma_start(x_tok[:, c * T:(c + 1) * T, :],
                                 x[bass.ds(b, 1), c * CH:(c + 1) * CH, :].rearrange("o (t p) f -> p (o t) f", p=P)).then_inc(s_x[c], 16)
                wait_before(sp, b, s_norm, 2 * LN_N)
                wait_before(sp, b, s_wmod, 4)
                wait_before(sp, b, s_res, 8)
                for r, row in enumerate((H1, G1, H2, G2, GS, GF, GSB, GFB)):
                    sp.dma_start(vec[:, r, :], mod_dram[bass.ds(b, 1), row, :].broadcast_to([P, C])).then_inc(s_vec, 16)
                for c in range(NCH):
                    for fc in range(KC):
                        n = c * KC + fc
                        sp.wait_ge(s_q_lo, b * Q_N + n + 1)
                        for part in range(2):
                            sp.dma_start(q_dram[part, fc * P:(fc + 1) * P, c * CH:(c + 1) * CH],
                                         actT["C"][part][:, n % 2, :].bitcast(F32)).then_inc(s_q_out[c], 16)

                def run(p, s, seen):
                    def load_rows(dram, part, heads, n0, n, dst, signal):
                        sp.dma_start(dst.bitcast(F32), dram[part, heads.start * D:heads.stop * D, n0:n0 + n]
                                     .rearrange("(h d) n -> d h n", d=D)).then_inc(signal, 16)

                    for step in p.order():
                        if step[0] == "k":
                            n = step[1]
                            fc, blk = divmod(n, p.blocks)
                            at = N - p.keys + blk * p.block
                            sp.wait_ge(s.k_lo, seen * (KC * p.blocks) + n + 1)
                            for part in range(2):
                                sp.dma_start(k_dram[part, fc * P:(fc + 1) * P, at:at + p.block],
                                             actT["C"][part][:, n % 2, 0:p.block].bitcast(F32)).then_inc(s.k_out, 16)
                        elif step[0] == "ka":
                            u = step[1]
                            if u == 0:
                                sp.wait_ge(s.k_out, seen * (32 * KC * p.blocks) + 32 * KC * p.blocks)
                            else:
                                sp.wait_ge(s.s2, seen * (UNITS * p.n2) + u * p.n2)
                            alone(sp)
                            first = (u % NG) * HG if p.heads == HG else 0
                            heads = range(first, first + p.heads)
                            kav = ka[:, :].rearrange("r (h n) -> r h n", h=p.heads)
                            for row, part in ((ROW_A, 0), (ROW_B, 1), (ROW_C, 0)):
                                load_rows(k_dram, part, heads, N - p.keys, p.keys, kav[row:row + D, :, :], s.ka)
                            sp.dma_start(kav[ROW_MASK:ROW_MASK + 1, :, :].bitcast(F32),
                                         neg_dram[bass.ds(b, 1), N - p.keys:N].rearrange("(o i) n -> o i n", i=1)
                                         .broadcast_to([1, p.heads, p.keys])).then_inc(s.ka, 16)
                        elif step[0] == "qa":
                            u = step[1]
                            c, g, slot = u // NG, u % NG, u % QSLOTS
                            if u % NG == 0 or u == 0:
                                sp.wait_ge(s_q_out[c], b * (32 * KC) + 32 * KC)
                                alone(sp)
                            if u >= QSLOTS:
                                sp.wait_ge(s.s2, seen * (UNITS * p.n2) + (u - QSLOTS + 1) * p.n2)
                            for row, part in ((ROW_A, 0), (ROW_B, 0), (ROW_C, 1)):
                                load_rows(q_dram, part, range(g * HG, (g + 1) * HG), c * CH, CH,
                                          qa[row:row + D, slot, :, :], s.qa[slot])
                        elif step[0] == "mT":
                            u = step[1]
                            slot = u % QSLOTS
                            sp.wait_ge(s.mT_sb, seen * UNITS + u + 1)
                            for part in range(2):
                                sp.dma_start(qa[ROW_MAX + part:ROW_MAX + part + 1, slot, :, :].bitcast(F32)
                                             .rearrange("r h (t q) -> r (h t) q", q=P),
                                             m_rows[part * HG * T:(part + 1) * HG * T, u % 2, :].bitcast(F32)).then_inc(s.m[slot], 16)

                by_path(sp, b, seen, run)
                for c in range(NCH):
                    sp.wait_ge(s_tok_free, b * (TOK_N // 2) + (TOK_AT["ff", c] + T) // 2)
                    alone(sp)
                    sp.dma_start(out[bass.ds(b, 1), c * CH:(c + 1) * CH, :].rearrange("o (t p) f -> p (o t) f", p=P),
                                 o_tok[:, :, :] if c == 0 else a_tok[1]).then_inc(s_out[c], 16)

            batches(sp, body)
            for c in range(NCH):
                sp.wait_ge(s_out[c], 16 * B)

        @block.gpsimd
        def _(pool):
            pool.memset(ident[:, :], 0.0).then_inc(s_ident, 1)
            pool.wait_ge(s_ident, 1)
            pool.affine_select(out=ident[:, :], in_=ident[:, :], compare_op=ALU.not_equal, fill=1.0, base=0,
                               pattern=[[-1, P]], channel_multiplier=1).then_inc(s_ident, 1)
            for tile, value in ((mhalf, -0.5), (eps0, EPS0), (eps1, EPS1)):
                pool.memset(tile[:, :], value).then_inc(s_const, 1)

            def split(src, hi, lo, value, signal, count):
                pool.tensor_copy(hi, src).then_inc(signal, 1)
                pool.wait_ge(signal, value + 1)
                return pool.tensor_tensor(lo, src, hi.bitcast(F32), ALU.subtract).then_inc(signal, 1)

            def staged(n):
                return stage[:, 0:n]

            pool.wait_ge(s_upb, 1)
            pieces = []
            for name, dram in (("proj", proj_w), ("fc1", fc1_w), ("fc2", fc2_w)):
                chunks, n = weights[name][0].shape[1], weights[name][0].shape[2]
                step = min(chunks, 1024 // n) or 1
                pieces += [(name, dram, k, min(step, chunks - k), n) for k in range(0, chunks, step)]
            for i, (name, dram, k, m, n) in enumerate(pieces):
                raw = stage[:, 0:m * n].rearrange("p (k n) -> p k n", n=n)
                if i:
                    pool.wait_ge(s_split, 2 * i)
                pool.dma_start(raw, dram.rearrange("(k p) n -> p k n", p=P)[:, k:k + m, :]).then_inc(s_stage, 16)
                pool.wait_ge(s_stage, 16 * (i + 1))
                split(raw, weights[name][0][:, k:k + m, :], weights[name][1][:, k:k + m, :], 2 * i, s_split, 2)
            n_stage = len(pieces)
            pool.wait_ge(s_split, 2 * n_stage)

            def body(b, seen):
                mods = (("ssm1", ssm_w1, 1, None), ("ssm2", ssm_w2, None, 4), ("ff1", ff_w1, 3, None), ("ff2", ff_w2, None, 5))
                wait_before(pool, b, s_tok_mm, TOK_N)
                pool.wait_ge(s_vec, b * 128 + 128)
                alone(pool)
                pool.wait_ge(s_cols, 32 + 16 * 8)
                at = 0
                for i, (name, dram, col, row) in enumerate(mods):
                    chunks, n = weights[name][0].shape[1], weights[name][0].shape[2]
                    raw = stage[:, 0:chunks * n].rearrange("p (k n) -> p k n", n=n)
                    if i:
                        pool.wait_ge(s_wmod, b * 4 + i)
                        alone(pool)
                    pool.dma_start(raw, dram.rearrange("(k p) n -> p k n", p=P)).then_inc(s_stage, 16)
                    pool.wait_ge(s_stage, 16 * n_stage + b * 64 + 16 * (i + 1))
                    factor = [cols[:, k, col, bass.ds(b, 1)].broadcast_to([P, n]) if row is None else vec[:, row, :]
                              for k in range(chunks)]
                    for k in range(chunks):
                        pool.tensor_tensor(weights[name][0][:, k, :], raw[:, k, :], factor[k], ALU.mult).then_inc(s_poolw, 1)
                    at += chunks
                    pool.wait_ge(s_poolw, b * 20 + at)
                    alone(pool)
                    for k in range(chunks):
                        pool.tensor_tensor(raw[:, k, :], raw[:, k, :], factor[k], ALU.mult).then_inc(s_poolw, 1)
                    at += chunks
                    pool.wait_ge(s_poolw, b * 20 + at)
                    pool.tensor_tensor(weights[name][1][:, :, :], raw, weights[name][0][:, :, :].bitcast(F32), ALU.subtract)\
                        .then_inc(s_wmod, 1)

                def shift(n, c, row):
                    xc = x_tok[:, c * T:(c + 1) * T, :]
                    pool.tensor_tensor(xc, xc, vec[:, row, :].rearrange("p (o c) -> p o c", o=1).broadcast_to([P, T, C]),
                                       ALU.add).then_inc(s_res, 1)

                def inverse_std(step, eps):
                    for pair in range(2):
                        n = LN_AT[step] + pair
                        pool.wait_ge(s_aggr, b * (2 * LN_N) + 2 * (n + 1))
                        pool.tensor_tensor(veps[:, n % 4, :], mv[:, n % 4, :, 1], eps, ALU.add).then_inc(s_eps, 1)
                        pool.wait_ge(s_eps, b * LN_N + n + 1)
                        pool.tensor_tensor(rstd[:, n % 4, :], veps[:, n % 4, :], mhalf[:, :], ALU.pow).then_inc(s_rstd, 1)

                def low_part(step, j):
                    n = H_AT[step] + j
                    pool.wait_ge(s_h_hi, b * H_N + n + 1)
                    pool.tensor_tensor(hid[:, n % HSLOTS, 1, :], gelu_out[:, n % 2, :], hid[:, n % HSLOTS, 0, :].bitcast(F32),
                                       ALU.subtract).then_inc(s_h_lo, 1)

                for c in range(NCH):
                    pool.wait_ge(s_t_mm, b * T_N + T_AT["x", c] + 2)
                    shift(c, c, 0)
                pool.wait_ge(s_const, 3)
                inverse_std(("proj", 0), eps0[:, :])
                inverse_std(("proj", 1), eps0[:, :])
                pool.wait_ge(s_t_mm, b * T_N + T_AT["T1", 0] + 2)
                shift(2, 0, 2)
                for j in range(HIDDEN["fc"]):
                    low_part(("fc", 0), j)
                pool.wait_ge(s_t_mm, b * T_N + T_AT["T1", 1] + 2)
                shift(3, 1, 2)
                low_part(("fc", 1), 0)
                inverse_std(("fc", 0), eps0[:, :])
                for j in (1, 2):
                    low_part(("fc", 1), j)
                inverse_std(("T2", 0), eps1[:, :])
                for j in range(3, HIDDEN["fc"]):
                    low_part(("fc", 1), j)
                pool.wait_ge(s_norm, b * (2 * LN_N) + 2 * (LN_AT["T2", 0] + 2))
                shift(4, 0, 6)
                inverse_std(("fc", 1), eps0[:, :])
                for j in range(HIDDEN["ssm"]):
                    low_part(("ssm", 0), j)
                inverse_std(("T2", 1), eps1[:, :])
                pool.wait_ge(s_norm, b * (2 * LN_N) + 2 * (LN_AT["T2", 1] + 2))
                shift(5, 1, 6)
                inverse_std(("T3", 0), eps1[:, :])
                for j in range(HIDDEN["ssm"]):
                    low_part(("ssm", 1), j)
                pool.wait_ge(s_norm, b * (2 * LN_N) + 2 * (LN_AT["T3", 0] + 2))
                shift(6, 0, 7)
                inverse_std(("T3", 1), eps1[:, :])
                for j in range(HIDDEN["ff"]):
                    low_part(("ff", 0), j)
                pool.wait_ge(s_norm, b * (2 * LN_N) + 2 * (LN_AT["T3", 1] + 2))
                shift(7, 1, 7)
                for j in range(HIDDEN["ff"]):
                    low_part(("ff", 1), j)

            with pool.Fori(0, B) as b:
                body(b, None)

        @block.scalar
        def _(act):
            act.wait_ge(s_cond, 16 * (B + 2))
            act.activation(silu1[:, :, :], condT[:, :, :], ACT.Silu).then_inc(s_silu, 1)
            act.wait_ge(s_ada_mm, 1)
            for f in range(KC):
                act.activation(silu0[:, f, :], ps[:, BANK_FEAT, f * B:(f + 1) * B], ACT.Silu, bias=ada1b[:, f:f + 1])\
                    .then_inc(s_silu, 1)
            act.wait_ge(s_qkv_raw, 16)
            act.activation(weights["qkv"][0][:, :, :], qkv_raw, ACT.Identity).then_inc(s_qkv_hi, 1)

            def body(b, seen):
                def high(step, slot):
                    for pair in range(T // 2):
                        n = T_AT[step] + pair
                        act.wait_ge(s_t_mm, b * T_N + n + 1)
                        act.activation(actT[slot][0][:, :, pair * C:(pair + 1) * C],
                                       ps[:, t_bank(n), :].rearrange("p (k n) -> p k n", k=KC), ACT.Identity)\
                           .then_inc(s_t_hi, 1)

                wait_before(act, b, s_tok_mm, TOK_N)
                high(("x", 0), "A")
                high(("x", 1), "B")
                for n in range(Q_N):
                    act.wait_ge(s_q_mm, b * Q_N + n + 1)
                    if n >= 2:
                        act.wait_ge(s_q_out[0], b * (32 * KC) + 32 * KC)
                    act.activation(actT["C"][0][:, n % 2, :], ps[:, BANK_FEAT + n % 2, :], ACT.Identity).then_inc(s_q_hi, 1)

                def run(p, s, seen):
                    for step in p.order():
                        if step[0] == "k":
                            n = step[1]
                            act.wait_ge(s.k_mm, seen * (KC * p.blocks) + n + 1)
                            if n == 0:
                                act.wait_ge(s_q_out[1], b * (32 * KC) + 32 * KC)
                            if n == 2:
                                act.wait_ge(s.k_out, seen * (32 * KC * p.blocks) + 64)
                            if n == 3:
                                pass
                            act.activation(actT["C"][0][:, n % 2, 0:p.block], ps[:, BANK_FEAT + n % 2, 0:p.block], ACT.Identity)\
                               .then_inc(s.k_hi, 1)
                        elif step[0] == "mT":
                            u = step[1]
                            act.wait_ge(s.mT, seen * UNITS + u + 1)
                            if u >= 2:
                                act.wait_ge(s.m[(u - 2) % QSLOTS], seen * (32 * slot_total(u - 2)) + 32 * slot_uses(u - 2))
                            act.activation(m_rows[:, u % 2, :], ps[0:2 * HG * T, BANK_T, 0:P], ACT.Identity).then_inc(s.mT_sb, 1)
                        elif step[0] == "s2":
                            _, u, kt, hp = step
                            n, v = u * p.n2 + 2 * kt + hp, u * p.kt + kt
                            act.wait_ge(s.s2, seen * (UNITS * p.n2) + n + 1)
                            if v >= 2:
                                act.wait_ge(s.pv, seen * (UNITS * p.kt) + v - 1)
                            act.activation(probs[:, kt % 2, 2 * hp:2 * hp + 2, :], ps[:, 2 * hp:2 * hp + 2, :], ACT.Exp,
                                           scale=SCALE).then_inc(s.exp, 1)
                        elif step[0] == "o":
                            u = step[1]
                            act.wait_ge(s.pv, seen * (UNITS * p.kt) + (u + 1) * p.kt)
                            if u >= 2:
                                act.wait_ge(s.oT, seen * UNITS + u - 1)
                            act.activation(o_sb[:, u % 2, :], ps[:, BANK_PV, :], ACT.Identity).then_inc(s.o_sb, 1)
                        elif step[0] == "attnT":
                            high(("o", step[1]), "AB"[step[1]])

                by_path(act, b, seen, run)
                bias = {"fc": lambda j: fc1b[:, j:j + 1], "ssm": lambda j: upb_mod[:, j, bass.ds(b, 1)],
                        "ff": lambda j: upb_mod[:, C // P + j, bass.ds(b, 1)]}
                for step in MLP_ORDER:
                    if step[0][0] == "T":
                        high(step, "CA"[step[1]])
                    elif step[0] in HIDDEN:
                        for j in range(HIDDEN[step[0]]):
                            n = H_AT[step] + j
                            act.wait_ge(s_up_mm, b * H_N + n + 1)
                            if n >= 2:
                                act.wait_ge(s_h_lo, b * H_N + n - 1)
                            alone(act)
                            act.activation(gelu_out[:, n % 2, :], ps[:, BANK_FEAT + n % 2, :],
                                           ACT.Gelu_apprx_tanh if step[0] == "ff" else ACT.Gelu, bias=bias[step[0]](j))\
                               .then_inc(s_gelu, 1)
                            act.wait_ge(s_gelu, b * H_N + n + 1)
                            if n >= HSLOTS:
                                act.wait_ge(s_h_used, b * H_N + n - HSLOTS + 1)
                            act.activation(hid[:, n % HSLOTS, 0, :], gelu_out[:, n % 2, :], ACT.Identity).then_inc(s_h_hi, 1)

            act.wait_ge(s_upb, 2)
            act.wait_ge(s_small, 16 * 7)
            batches(act, body)

        @block.vector
        def _(dve):
            dve.wait_ge(s_mask, 32)
            dve.tensor_copy(mask_f, mask_rows[:, :]).then_inc(s_dset, 1)
            dve.wait_ge(s_dset, 1)
            dve.tensor_scalar(mask_neg[:, :], mask_f, 1.0, -MASKED, ALU.subtract, ALU.mult).then_inc(s_dset, 1)
            dve.tensor_reduce(flags[0:1, 0:B], mask_line[:, :, 0:N - FAST.keys], axis=AX.X, op=ALU.max).then_inc(s_flags, 1)
            dve.wait_ge(s_flags, 1)
            dve.tensor_scalar(flags[0:1, B:2 * B], flags[0:1, 0:B], -1.0, 1.0, ALU.mult, ALU.add).then_inc(s_flags, 1)
            qz = qa[:, :, :, :].rearrange("r s h n -> r (s h n)")
            dve.memset(qz[32:64, :].bitcast(F32), 0.0).then_inc(s_dset, 1)
            dve.memset(qz[64:96, :].bitcast(F32), 1.0).then_inc(s_dset, 1)
            dve.memset(ka[32:64, :].bitcast(F32), 0.0).then_inc(s_dset, 1)
            dve.memset(ka[64:96, :].bitcast(F32), 0.0).then_inc(s_dset, 1)
            dve.memset(ka[96:98, :].bitcast(F32), 1.0).then_inc(s_dset, 1)
            dve.memset(ps[:, BANK_PV, :], 0.0).then_inc(s_dset, 1)
            dve.wait_ge(s_maskT, 1)
            dve.tensor_copy(mask_col[:, :], ps[:, BANK_T, 0:B * N // P]).then_inc(s_dset, 1)
            dve.wait_ge(s_qkv_hi, 1)
            dve.tensor_tensor(weights["qkv"][1][:, :, :], qkv_raw, weights["qkv"][0][:, :, :].bitcast(F32), ALU.subtract)\
               .then_inc(s_qkv_lo, 1)
            for layer in range(2):
                base = 5 * layer
                dve.wait_ge(s_ada_mm, 2 + layer)
                dve.wait_ge(s_bias_row[layer], 16)
                if layer:
                    dve.wait_ge(s_mod_out, 16)
                dve.tensor_tensor(ada_row[:, 0:6, :], ps[0:B, 0:3, :].rearrange("b a (r c) -> b (a r) c", c=C), bias_row,
                                  ALU.add).then_inc(s_ada_row, 1)
                dve.wait_ge(s_ada_row, base + 1)
                if layer == 0:
                    for i, half in enumerate((0, 3)):
                        shift, scale, gate = [ada_row[:, half + r, :] for r in range(3)]
                        dve.tensor_tensor(shift, shift, gate, ALU.mult).then_inc(s_ada_row, 1)
                        dve.scalar_tensor_tensor(out=scale, in0=scale, scalar=1.0, in1=gate, op0=ALU.add, op1=ALU.mult)\
                           .then_inc(s_ada_row, 1)
                else:
                    dve.wait_ge(s_small, 16 * 7)
                    for i, half in enumerate((0, 3)):
                        scale, gate = ada_row[:, half + 1, :], ada_row[:, half + 2, :]
                        dve.tensor_scalar(scale, scale, 1.0, None, ALU.add).then_inc(s_ada_row, 1)
                        dve.tensor_tensor(ada_row[:, 6 + i, :], gate, down_b_row[:, i, :], ALU.mult).then_inc(s_ada_row, 1)
            dve.wait_ge(s_upb, 1)
            dve.tensor_tensor(upb_mod[:, :, :], ps[:, BANK_FEAT, 0:6 * B].rearrange("p (f b) -> p f b", b=B),
                              upb[:, :].rearrange("p (f o) -> p f o", o=1).broadcast_to([P, 6, B]), ALU.add).then_inc(s_upb, 1)

            def body(b, seen):
                def low(step, slot):
                    for pair in range(T // 2):
                        n = T_AT[step] + pair
                        cs = slice(pair * C, (pair + 1) * C)
                        dve.wait_ge(s_t_hi, b * T_N + n + 1)
                        dve.tensor_tensor(actT[slot][1][:, :, cs], ps[:, t_bank(n), :].rearrange("p (k n) -> p k n", k=KC),
                                          actT[slot][0][:, :, cs].bitcast(F32), ALU.subtract).then_inc(s_t_lo, 1)

                low(("x", 0), "A")
                low(("x", 1), "B")
                for n in range(Q_N):
                    dve.wait_ge(s_q_hi, b * Q_N + n + 1)
                    dve.tensor_tensor(actT["C"][1][:, n % 2, :], ps[:, BANK_FEAT + n % 2, :],
                                      actT["C"][0][:, n % 2, :].bitcast(F32), ALU.subtract).then_inc(s_q_lo, 1)

                def run(p, s, seen):
                    for step in p.order():
                        if step[0] == "k":
                            n = step[1]
                            dve.wait_ge(s.k_hi, seen * (KC * p.blocks) + n + 1)
                            dve.tensor_tensor(actT["C"][1][:, n % 2, 0:p.block], ps[:, BANK_FEAT + n % 2, 0:p.block],
                                              actT["C"][0][:, n % 2, 0:p.block].bitcast(F32), ALU.subtract).then_inc(s.k_lo, 1)
                        elif step[0] == "v":
                            n = step[1]
                            at = (N - p.keys) // P + n
                            m = mask_col[:, bass.ds(b * (N // P) + at, 1)]
                            dve.wait_ge(s.v_mm, seen * p.kt + n + 1)
                            dve.tensor_scalar(v_sb[:, n, :, 0:D],
                                              ps[:, BANK_TOK + n % 4, 0:C].rearrange("p (h d) -> p h d", d=D),
                                              m, None, ALU.mult).then_inc(s.v, 1)
                            dve.tensor_copy(v_sb[:, n, :, D], m.broadcast_to([P, H])).then_inc(s.v, 1)
                        elif step[0] == "s1":
                            _, u, i = step
                            n = u * p.n1 + i
                            dve.wait_ge(s.s1, seen * (UNITS * p.n1) + n + 1)
                            bank = ps[:, BANK_TOK + 2 + n % 2, :]
                            if p is FAST:
                                h, tp = divmod(i, T // 2)
                                if i == 0 and u >= 2:
                                    dve.wait_ge(s.neg, seen * (2 * UNITS) + 2 * (u - 1))
                                dve.tensor_reduce(mmax[:, u % 2, h * T + 2 * tp:h * T + 2 * tp + 2],
                                                  bank.rearrange("p (t n) -> p t n", t=2), axis=AX.X, op=ALU.max).then_inc(s.max, 1)
                            else:
                                h, t, half = i // (2 * T), i // 2 % T, i % 2
                                dve.tensor_reduce(mpart[:, u % 2, h, t, half:half + 1], bank, axis=AX.X, op=ALU.max)\
                                   .then_inc(s.max, 1)
                        elif step[0] == "mneg":
                            u = step[1]
                            dve.wait_ge(s.max, seen * (UNITS * p.n1) + (u + 1) * p.n1)
                            if p is FULL:
                                dve.tensor_reduce(mmax[:, u % 2, :], mpart[:, u % 2, :, :, :].rearrange("p h t a -> p (h t) a"),
                                                  axis=AX.X, op=ALU.max).then_inc(s.fold, 1)
                                dve.wait_ge(s.fold, seen * UNITS + u + 1)
                            if u >= 2:
                                dve.wait_ge(s.mT, seen * UNITS + u - 1)
                            hi, lo = mhl[:, u % 2, 0:HG * T], mhl[:, u % 2, HG * T:2 * HG * T]
                            dve.tensor_scalar(hi, mmax[:, u % 2, :], -1.0, None, ALU.mult).then_inc(s.neg, 1)
                            dve.wait_ge(s.neg, seen * (2 * UNITS) + 2 * u + 1)
                            dve.scalar_tensor_tensor(out=lo, in0=mmax[:, u % 2, :], scalar=-1.0, in1=hi.bitcast(F32),
                                                     op0=ALU.mult, op1=ALU.subtract).then_inc(s.neg, 1)
                        elif step[0] == "oT":
                            u = step[1]
                            c, g = u // NG, u % NG
                            if u == 0:
                                alone(dve)
                                wait_before(dve, b, s_out[0], 16)
                            dve.wait_ge(s.oT, seen * UNITS + u + 1)
                            if c and g == 0:
                                dve.wait_ge(s_t_mm, b * T_N + T_AT["o", c - 1] + 2)
                            if u >= 1:
                                dve.wait_ge(s.o, seen * UNITS + u)
                            bank = ps[:, BANK_T, :].rearrange("p (t h d) -> p t h d", t=T, h=HG)
                            dve.reciprocal(rden[:, :, :], bank[:, :, :, D]).then_inc(s.rden, 1)
                            dve.wait_ge(s.rden, seen * UNITS + u + 1)
                            dve.tensor_tensor(o_tok[:, :, g * HG * D:(g + 1) * HG * D].rearrange("p t (h d) -> p t h d", d=D),
                                              bank[:, :, :, 0:D],
                                              rden[:, :, :].rearrange("p t (h o) -> p t h o", o=1).broadcast_to([P, T, HG, D]),
                                              ALU.mult).then_inc(s.o, 1)
                        elif step[0] == "attnT":
                            low(("o", step[1]), "AB"[step[1]])

                by_path(dve, b, seen, run)

                def statistics(n, tiles):
                    for t in range(2):
                        if n:
                            dve.wait_ge(s_aggr, b * (2 * LN_N) + 2 * (n - 1) + t + 1)
                        dve.bn_stats(stats[:, t, :], tiles[t]).then_inc(s_bn, 1)
                    for t in range(2):
                        dve.wait_ge(s_bn, b * (2 * LN_N) + 2 * n + t + 1)
                        alone(dve)
                        dve.bn_aggr(mv[:, n % 4, t, :], stats[:, t, :]).then_inc(s_aggr, 1)

                def ln_in(step, bias):
                    for pair in range(2):
                        tok, n = TOK_AT[step] + 2 * pair, LN_AT[step] + pair
                        dve.wait_ge(s_tok_mm, b * TOK_N + tok + 2)
                        a = a_tok[step[1]][:, 2 * pair:2 * pair + 2, :]
                        bank = BANK_TOK + tok % 4
                        dve.tensor_tensor(a, ps[:, bank:bank + 2, 0:C],
                                          vec[:, bias, :].rearrange("p (o c) -> p o c", o=1).broadcast_to([P, 2, C]), ALU.add)\
                           .then_inc(s_tok_free, 1)
                        dve.wait_ge(s_tok_free, b * (TOK_N // 2) + tok // 2 + 1)
                        statistics(n, [a[:, t, :] for t in range(2)])

                def ln_apply(step, gain):
                    for pair in range(2):
                        n = LN_AT[step] + pair
                        dve.wait_ge(s_aggr, b * (2 * LN_N) + 2 * (n + 1))
                        for t in range(2):
                            a = a_tok[step[1]][:, 2 * pair + t, :]
                            dve.scalar_tensor_tensor(out=a, in0=a, scalar=mv[:, n % 4, t, 0:1], in1=vec[:, gain, :],
                                                     op0=ALU.subtract, op1=ALU.mult).then_inc(s_cen, 1)
                    for pair in range(2):
                        n = LN_AT[step] + pair
                        dve.wait_ge(s_rstd, b * LN_N + n + 1)
                        for t in range(2):
                            a = a_tok[step[1]][:, 2 * pair + t, :]
                            xt = x_tok[:, step[1] * T + 2 * pair + t, :]
                            dve.wait_ge(s_cen, b * 16 + CEN_AT[step] + 2 * pair + t + 1)
                            dve.scalar_tensor_tensor(out=xt, in0=a, scalar=rstd[:, n % 4, t:t + 1], in1=xt,
                                                     op0=ALU.mult, op1=ALU.add).then_inc(s_norm, 1)

                def z_in(step, ready):
                    for pair in range(2):
                        ready(pair)
                        statistics(LN_AT[step] + pair, [x_tok[:, step[1] * T + 2 * pair + t, :] for t in range(2)])

                def z_apply(step):
                    for pair in range(2):
                        n = LN_AT[step] + pair
                        dve.wait_ge(s_rstd, b * LN_N + n + 1)
                        for t in range(2):
                            dve.tensor_scalar(a_tok[step[1]][:, 2 * pair + t, :], x_tok[:, step[1] * T + 2 * pair + t, :],
                                              mv[:, n % 4, t, 0:1], rstd[:, n % 4, t:t + 1], ALU.subtract, ALU.mult).then_inc(s_norm, 1)

                def add_residual(step, dst):
                    for pair in range(2):
                        tok = TOK_AT[step] + 2 * pair
                        ts = slice(2 * pair, 2 * pair + 2)
                        bank = BANK_TOK + tok % 4
                        dve.wait_ge(s_tok_mm, b * TOK_N + tok + 2)
                        dve.tensor_tensor(dst[:, ts, :], ps[:, bank:bank + 2, 0:C],
                                          x_tok[:, step[1] * T + 2 * pair:step[1] * T + 2 * pair + 2, :], ALU.add)\
                           .then_inc(s_tok_free, 1)

                def after_norm(step):
                    def ready(pair):
                        dve.wait_ge(s_norm, b * (2 * LN_N) + 2 * LN_AT[step] + 2 * pair + 2)
                    return ready

                def after_add(step):
                    def ready(pair):
                        dve.wait_ge(s_tok_free, b * (TOK_N // 2) + TOK_AT[step] // 2 + pair + 1)
                    return ready

                def res(n):
                    dve.wait_ge(s_res, b * 8 + n)

                def a_free(step):
                    dve.wait_ge(s_t_mm, b * T_N + T_AT[step] + 2)

                x_chunk = [x_tok[:, c * T:(c + 1) * T, :] for c in range(NCH)]
                wait_before(dve, b, s_out[1], 16)
                dve.wait_ge(s_vec, b * 128 + 128)
                ln_in(("proj", 0), 8)
                res(2)
                ln_apply(("proj", 0), 1)
                ln_in(("proj", 1), 8)
                low(("T1", 0), "C")
                ln_apply(("proj", 1), 1)
                low(("T1", 1), "A")
                dve.wait_ge(s_norm, b * (2 * LN_N) + 2 * (LN_AT["proj", 1] + 2))
                ln_in(("fc", 0), 9)
                res(4)
                ln_apply(("fc", 0), 3)
                z_in(("T2", 0), after_norm(("fc", 0)))
                z_apply(("T2", 0))
                low(("T2", 0), "C")
                ln_in(("fc", 1), 9)
                ln_apply(("fc", 1), 3)
                z_in(("T2", 1), after_norm(("fc", 1)))
                z_apply(("T2", 1))
                low(("T2", 1), "A")
                res(5)
                add_residual(("ssm", 0), x_chunk[0])
                z_in(("T3", 0), after_add(("ssm", 0)))
                z_apply(("T3", 0))
                low(("T3", 0), "C")
                res(6)
                add_residual(("ssm", 1), x_chunk[1])
                z_in(("T3", 1), after_add(("ssm", 1)))
                z_apply(("T3", 1))
                low(("T3", 1), "A")
                res(7)
                add_residual(("ff", 0), o_tok)
                res(8)
                add_residual(("ff", 1), a_tok[1])

            CEN_AT = {("proj", 0): 0, ("proj", 1): 4, ("fc", 0): 8, ("fc", 1): 12}
            batches(dve, body)

        @block.tensor
        def _(pe):
            def product(dst, left, right, start=True, stop=True):
                n = len(left[0])
                for k in range(n):
                    for i, (a, w) in enumerate(((0, 0), (0, 1), (1, 0))):
                        last = pe.matmul(dst, left[a][k], right[w][k], start=start and k == 0 and i == 0,
                                         stop=stop and k == n - 1 and i == 2)
                return last

            pe.wait_ge(s_ident, 2)
            pe.wait_ge(s_dset, 1)
            pe.transpose(ps[:, BANK_T, 0:B * N // P], mask_f, ident[0:B * N // P, 0:B * N // P]).then_inc(s_maskT, 1)
            pe.wait_ge(s_cond, 16 * (B + 2))
            for f in range(KC):
                for k in range(KC):
                    last = pe.matmul(ps[:, BANK_FEAT, f * B:(f + 1) * B], ada1_raw[:, k, f * P:(f + 1) * P], condT[:, k, :],
                                     start=k == 0, stop=k == KC - 1)
            last.then_inc(s_ada_mm, 1)
            for layer, silu in enumerate((silu0, silu1)):
                pe.wait_ge(s_silu, 3)
                pe.wait_ge(s_ada_raw[layer], 16)
                if layer:
                    pe.wait_ge(s_ada_row, 1)
                for n in range(3):
                    for k in range(KC):
                        last = pe.matmul(ps[0:B, n, :], silu[:, k, :], ada_raw[:, k, n * CH:(n + 1) * CH],
                                         start=k == 0, stop=k == KC - 1)
                last.then_inc(s_ada_mm, 1)
            pe.wait_ge(s_cols, 32 + 16 * 8)
            pe.wait_ge(s_ada_row, 6)
            up = [(stage[:, 0:2 * C].rearrange("p (k n) -> p k n", k=KC), 0, f) for f in range(C // P)] + \
                 [(stage[:, 2 * C:6 * C].rearrange("p (k n) -> p k n", k=KC), 2, f) for f in range(FF1 // P)]
            for i, (w, shift, f) in enumerate(up):
                for k in range(KC):
                    last = pe.matmul(ps[:, BANK_FEAT, i * B:(i + 1) * B], w[:, k, f * P:(f + 1) * P], cols[:, k, shift, :],
                                     start=k == 0, stop=k == KC - 1)
            last.then_inc(s_upb, 1)
            pe.wait_ge(s_upb, 2)
            pe.wait_ge(s_dset, 9)
            pe.wait_ge(s_qkv_lo, 1)

            def body(b, seen):
                def transpose_pair(n, tiles):
                    for t in range(2):
                        for k in range(KC):
                            last = pe.transpose(ps[:, t_bank(n), (2 * k + t) * P:(2 * k + t + 1) * P],
                                                tiles[t][:, k * P:(k + 1) * P], ident[:, :])
                    last.then_inc(s_t_mm, 1)

                def transposes(step, src):
                    for pair in range(2):
                        n = T_AT[step] + pair
                        if t_before(n) >= 0:
                            pe.wait_ge(s_t_lo, b * T_N + t_before(n) + 1)
                        transpose_pair(n, [src[:, 2 * pair + t, :] for t in range(2)])

                for c in range(NCH):
                    pe.wait_ge(s_x[c], b * 16 + 16)
                    transposes(("x", c), x_tok[:, c * T:(c + 1) * T, :])
                for c in range(NCH):
                    pe.wait_ge(s_t_lo, b * T_N + T_AT["x", c] + 2)
                    for fc in range(KC):
                        n = c * KC + fc
                        if n >= 2:
                            pe.wait_ge(s_q_lo, b * Q_N + n - 1)
                        fs = slice(fc * P, (fc + 1) * P)
                        product(ps[:, BANK_FEAT + n % 2, :],
                                [[weights["qkv"][part][:, k, fs] for k in range(KC)] for part in range(2)],
                                [x_tile(None, part, c * CH, CH) for part in range(2)]).then_inc(s_q_mm, 1)

                def run(p, s, seen):
                    bank_t = None

                    def take_bank_t(sem_, value):
                        nonlocal bank_t
                        if bank_t is not None:
                            pe.wait_ge(*bank_t)
                        bank_t = (sem_, value)

                    kav = ka[:, :].rearrange("r (h n) -> r h n", h=p.heads)
                    for step in p.order():
                        if step[0] == "k":
                            n = step[1]
                            fc, blk = divmod(n, p.blocks)
                            if n < 2:
                                pe.wait_ge(s_q_lo, b * Q_N + Q_N - 1 + n)
                            else:
                                pe.wait_ge(s.k_lo, seen * (KC * p.blocks) + n - 1)
                            fs = slice(C + fc * P, C + (fc + 1) * P)
                            product(ps[:, BANK_FEAT + n % 2, 0:p.block],
                                    [[weights["qkv"][part][:, k, fs] for k in range(KC)] for part in range(2)],
                                    [x_tile(None, part, N - p.keys + blk * p.block, p.block) for part in range(2)])\
                                .then_inc(s.k_mm, 1)
                        elif step[0] == "v":
                            n = step[1]
                            if n >= 4:
                                pe.wait_ge(s.v, seen * (2 * p.kt) + 2 * (n - 3))
                            product(ps[:, BANK_TOK + n % 4, 0:C],
                                    [x_tile(None, part, N - p.keys + n * P, P) for part in range(2)],
                                    [[weights["qkv"][part][:, k, 2 * C:3 * C] for k in range(KC)] for part in range(2)])\
                                .then_inc(s.v_mm, 1)
                        elif step[0] == "s1":
                            _, u, i = step
                            n, slot = u * p.n1 + i, u % QSLOTS
                            if i == 0:
                                if u == 0:
                                    pe.wait_ge(s.v, seen * (2 * p.kt) + 2 * p.kt)
                                if u == 0 or p is FULL:
                                    pe.wait_ge(s.ka, seen * (64 * (UNITS if p is FULL else 1)) + 64 * (u + 1))
                                pe.wait_ge(s.qa[slot], seen * (48 * slot_total(u)) + 48 * slot_uses(u))
                            if n >= 2:
                                pe.wait_ge(s.max, seen * (UNITS * p.n1) + n - 1)
                            bank = BANK_TOK + 2 + n % 2
                            if p is FAST:
                                h, tp = divmod(i, T // 2)
                                for t in range(2):
                                    q0 = (2 * tp + t) * P
                                    last = pe.matmul(ps[:, bank, t * p.keys:(t + 1) * p.keys], qa[0:ROWS_S1, slot, h, q0:q0 + P],
                                                     kav[0:ROWS_S1, (u % NG) * HG + h, :], start=True, stop=True)
                            else:
                                h, t, half = i // (2 * T), i // 2 % T, i % 2
                                last = pe.matmul(ps[:, bank, :], qa[0:ROWS_S1, slot, h, t * P:(t + 1) * P],
                                                 kav[0:ROWS_S1, h, half * CH:(half + 1) * CH], start=True, stop=True)
                            last.then_inc(s.s1, 1)
                        elif step[0] == "mT":
                            u = step[1]
                            take_bank_t(s.mT_sb, seen * UNITS + u + 1)
                            pe.wait_ge(s.neg, seen * (2 * UNITS) + 2 * (u + 1))
                            pe.transpose(ps[0:2 * HG * T, BANK_T, 0:P], mhl[:, u % 2, :].bitcast(F32), ident[:, :]).then_inc(s.mT, 1)
                        elif step[0] == "s2":
                            _, u, kt, hp = step
                            n, slot = u * p.n2 + 2 * kt + hp, u % QSLOTS
                            if kt == 0 and hp == 0:
                                pe.wait_ge(s.m[slot], seen * (32 * slot_total(u)) + 32 * slot_uses(u))
                            if n >= 2:
                                pe.wait_ge(s.exp, seen * (UNITS * p.n2) + n - 1)
                            for h in (2 * hp, 2 * hp + 1):
                                head = (u % NG) * HG + h if p.heads == H else h
                                last = pe.matmul(ps[:, h, :], kav[0:ROWS_S2, head, kt * P:(kt + 1) * P], qa[0:ROWS_S2, slot, h, :],
                                                 start=True, stop=True)
                            last.then_inc(s.s2, 1)
                        elif step[0] == "pv":
                            _, u, kt = step
                            pe.wait_ge(s.exp, seen * (UNITS * p.n2) + u * p.n2 + 2 * (kt + 1))
                            if kt == 0 and u >= 1:
                                pe.wait_ge(s.o_sb, seen * UNITS + u)
                            for h in range(HG):
                                last = pe.matmul(ps[32 * h:32 * h + VW, BANK_PV, :], v_sb[:, kt, (u % NG) * HG + h, :],
                                                 probs[:, kt % 2, h, :], start=kt == 0, stop=kt == p.kt - 1)
                            last.then_inc(s.pv, 1)
                        elif step[0] == "oT":
                            u = step[1]
                            take_bank_t(s.o, seen * UNITS + u + 1)
                            pe.wait_ge(s.o_sb, seen * UNITS + u + 1)
                            for t in range(T):
                                last = pe.transpose(ps[:, BANK_T, t * P:(t + 1) * P], o_sb[:, u % 2, t * P:(t + 1) * P], ident[:, :])
                            last.then_inc(s.oT, 1)
                        elif step[0] == "attnT":
                            c = step[1]
                            pe.wait_ge(s.o, seen * UNITS + (c + 1) * NG)
                            for pair in range(2):
                                n = T_AT["o", c] + pair
                                take_bank_t(s_t_lo, b * T_N + n + 1)
                                transpose_pair(n, [o_tok[:, 2 * pair + t, :] for t in range(2)])

                by_path(pe, b, seen, run)

                def tok_tile(n):
                    return ps[:, BANK_TOK + n % 4, 0:C]

                def take_tok(n):
                    if n >= 4:
                        pe.wait_ge(s_tok_free, b * (TOK_N // 2) + (n - 4) // 2 + 1)

                up_w = {"fc": "fc1", "ssm": "ssm1", "ff": "ff1"}
                down_w = {"fc": "fc2", "ssm": "ssm2", "ff": "ff2"}

                def up(step, j, slot):
                    n = H_AT[step] + j
                    if n >= 2:
                        pe.wait_ge(s_gelu, b * H_N + n - 1)
                    w = weights[up_w[step[0]]]
                    product(ps[:, BANK_FEAT + n % 2, :],
                            [[w[part][:, k, j * P:(j + 1) * P] for k in range(KC)] for part in range(2)],
                            [[actT[slot][part][:, k, :] for k in range(KC)] for part in range(2)]).then_inc(s_up_mm, 1)

                def down(step, j):
                    n = H_AT[step] + j
                    w = weights[down_w[step[0]]]
                    pe.wait_ge(s_h_lo, b * H_N + n + 1)
                    for t in range(T):
                        tok = TOK_AT[step] + t
                        if j == 0:
                            take_tok(tok)
                        last = product(tok_tile(tok),
                                       [[hid[:, n % HSLOTS, part, t * P:(t + 1) * P]] for part in range(2)],
                                       [[w[part][:, j, :]] for part in range(2)],
                                       start=j == 0, stop=j == HIDDEN[step[0]] - 1)
                        if j == HIDDEN[step[0]] - 1:
                            last.then_inc(s_tok_mm, 1)
                    pe.nop().then_inc(s_h_used, 1) if j == HIDDEN[step[0]] - 1 else last.then_inc(s_h_used, 1)

                pe.wait_ge(s_split, 2 * 5)
                for step in MLP_ORDER:
                    kind, c = step
                    if kind == "proj":
                        pe.wait_ge(s_t_lo, b * T_N + T_AT["o", c] + 2)
                        for t in range(T):
                            n = TOK_AT[step] + t
                            take_tok(n)
                            product(tok_tile(n),
                                    [[actT["AB"[c]][part][:, k, t * P:(t + 1) * P] for k in range(KC)] for part in range(2)],
                                    [[weights["proj"][part][:, k, :] for k in range(KC)] for part in range(2)])\
                                .then_inc(s_tok_mm, 1)
                    elif kind == "T1":
                        for pair in range(2):
                            n = T_AT[step] + pair
                            if t_before(n) >= 0:
                                pe.wait_ge(s_t_lo, b * T_N + t_before(n) + 1)
                            pe.wait_ge(s_norm, b * (2 * LN_N) + 2 * (LN_AT["proj", c] + pair + 1))
                            transpose_pair(n, [x_tok[:, c * T + 2 * pair + t, :] for t in range(2)])
                    elif kind in ("T2", "T3"):
                        for pair in range(2):
                            n = T_AT[step] + pair
                            if t_before(n) >= 0:
                                pe.wait_ge(s_t_lo, b * T_N + t_before(n) + 1)
                            pe.wait_ge(s_norm, b * (2 * LN_N) + 2 * (LN_AT[step] + pair + 1))
                            transpose_pair(n, [a_tok[c][:, 2 * pair + t, :] for t in range(2)])
                    else:
                        slot = "CA"[c]
                        last_t = {"fc": "T1", "ssm": "T2", "ff": "T3"}[kind]
                        pe.wait_ge(s_t_lo, b * T_N + T_AT[last_t, c] + 2)
                        if kind != "fc" and c == 0:
                            pe.wait_ge(s_wmod, b * 4 + 4)
                        total = HIDDEN[kind]
                        for j in range(total + 2):
                            if j < total:
                                up(step, j, slot)
                            if j >= 2:
                                down(step, j - 2)

            batches(pe, body)


_INS = ["x", "cond_1024", "mask_BxS_bk0"] + \
    ["L0_cond_" + n for n in ("qkv_w", "proj_w", "proj_b", "fc1_w", "fc1_b", "fc2_w", "fc2_b", "ada1_w", "ada1_b", "ada2_w", "ada2_b")] + \
    ["L1_cond_" + n for n in ("ada_w", "ada_b", "ssm_w1", "ssm_b1", "ssm_w2", "ssm_b2", "ff_w1", "ff_b1", "ff_w2", "ff_b2")]


def kernel(**inputs):
    import numpy as np
    import concourse.bacc as bacc
    from concourse.bass_utils import run_bass_kernel_spmd

    nc = bacc.Bacc("TRN2", target_bir_lowering=False, num_devices=1, dynamic_dma_scratch_size=8192)
    arrays, args = {}, []
    for name in _INS:
        a = np.ascontiguousarray(inputs[name])
        arrays[f"in_{name}"] = a
        args.append(nc.dram_tensor(f"in_{name}", a.shape, mybir.dt.from_np(a.dtype), kind="ExternalInput").ap())
    args.append(nc.dram_tensor("out_0", (B, N, C), F32, kind="ExternalOutput").ap())
    build(nc, *args)
    r = run_bass_kernel_spmd(nc, [arrays], core_ids=[0])
    return r.results[0]["out_0"]
```

```python
from contextlib import ExitStack

import concourse.bass as bass
from concourse import mybir

F32 = mybir.dt.float32
F32R = mybir.dt.float32r
U8 = mybir.dt.uint8
I32 = mybir.dt.int32
ALU = mybir.AluOpType
ACT = mybir.ActivationFunctionType
AX = mybir.AxisListType

B, N, C = 2, 1024, 256
P = 128
H, D = 16, 16
KC = C // P
CH = 512
NCH = N // CH
T = CH // P
HG = 4
NG = H // HG
UNITS = NCH * NG
VW = D + 1
FF0, FF1 = 4 * C, 2 * C
MASKED = -1e30
SCALE = D ** -0.5
EPS0, EPS1 = 1e-5, 1e-6
SPLITS = 2 * (C * C + 2 * C * FF0) // (2 * C * P)
QK_BUFS = 5
QSLOTS = 3
HSLOTS = 3

ROW_A, ROW_B, ROW_C = 0, 16, 32
ROW_MASK = 64
ROW_MAX = 96
ROWS_S1, ROWS_S2 = 96, 98

BANK_FEAT, BANK_TOK, BANK_PV, BANK_T = 0, 2, 6, 7
ADA_BANK = 3, 0

H1, G1, H2, G2, GS, GF, GSB, GFB, SH_S, SC_S, SH_F, SC_F = range(12)


Q_N = KC * NCH


class Path:

    def __init__(self, name, keys):
        self.name, self.keys = name, keys
        self.kt = keys // P
        self.block = min(CH, keys)
        self.blocks = keys // self.block
        self.k_tiles = KC * self.blocks
        self.n1 = HG * T * keys // CH
        self.n2 = 2 * self.kt
        self.heads = H if keys * H <= 4096 else HG

    def order(self):
        if self.kt == 2:
            return self.skewed()
        steps = self.projections()
        for u in range(UNITS):
            steps += [("ka", u), ("qa", u)] + [("s1", u, n) for n in range(self.n1)]
            steps += [("adb", 1), ("ada", 1), ("rows", 1)] * (u == 0) + [("mneg", u), ("mT", u)]
            for kt in range(self.kt):
                steps += [("s2", u, kt, 0), ("s2", u, kt, 1)] + [("pv", u, kt - 1)] * (kt > 0)
            steps += [("pv", u, self.kt - 1), ("o", u), ("oT", u)]
            steps += [("attnT", u // NG)] * (u % NG == NG - 1)
        return steps + [("upb", 1)]

    def projected(self):
        return [step for step in self.projections() if step[0] in "kq"]

    def projections(self):
        steps = [("x", 0), ("q", 0), ("q", 1), ("x", 1)] + [("k", n) for n in range(self.k_tiles)] + [("q", 2), ("q", 3)]
        return steps + [("v", n) for n in range(self.kt)] + [("ada", 0), ("rows", 0)]

    def skewed(self):
        steps = self.projections()
        at = steps.index(("q", Q_N - 1))
        steps[at:at] = [("ka", 0), ("qa", 0)]
        steps += [("qa", u) for u in range(1, QSLOTS)] + [("adb", 1)]
        tiles = [(u, n) for u in range(UNITS) for n in range(self.n1)]
        after = None

        def s1():
            nonlocal after
            u, n = tiles.pop(0)
            out = [("s1", u, n)]
            if n == self.n1 - 1:
                out.append(("mneg", u))
                after = u
            return out

        def m_t():
            nonlocal after
            out = [] if after is None else [("mT", after)]
            after = None
            return out

        for _ in range(3 * self.n1 // 2):
            steps += s1()
            if tiles[0][1] == 2:
                steps += m_t()
        steps += [("ada", 1), ("rows", 1)]
        for u in range(UNITS):
            for i in range(self.n2):
                steps.append(("s2", u, i // 2, i % 2))
                for _ in range(self.n1 // self.n2):
                    steps += s1() if tiles else []
                if i == 1:
                    steps += [("pv", u - 1, 1), ("o", u - 1)] if u > 0 else []
                    steps += m_t()
                if i == 3:
                    steps.append(("pv", u, 0))
                    if u > 0:
                        steps.append(("oT", u - 1))
                        steps += [("attnT", (u - 1) // NG)] * ((u - 1) % NG == NG - 1)
            if u + QSLOTS < UNITS:
                steps.append(("qa", u + QSLOTS))
            steps += m_t()
        u = UNITS - 1
        return steps + [("pv", u, 1), ("o", u), ("oT", u), ("attnT", u // NG), ("upb", 1)]


FAST, FULL = Path("fast", 256), Path("full", N)

MLP_ORDER = [("proj", 0), ("proj", 1), ("T1", 0), ("fc", 0), ("T1", 1), ("fc", 1), ("T2", 0),
             ("ssm", 0), ("T2", 1), ("ssm", 1), ("T3", 0), ("ff", 0), ("T3", 1), ("ff", 1)]
HIDDEN = {"fc": FF0 // P, "ssm": C // P, "ff": FF1 // P}


def numbered(kinds, each):
    at, n = {}, 0
    for step in kinds:
        at[step] = n
        n += each(step)
    return at, n


T_AT, T_N = numbered([("x", 0), ("x", 1), ("o", 0), ("o", 1)] + [s for s in MLP_ORDER if s[0][0] == "T"],
                     lambda s: T // 2)
MLPS = [s for s in MLP_ORDER if s[0] in HIDDEN]
H_AT, H_N = numbered(MLPS, lambda s: HIDDEN[s[0]])
TOK_AT, TOK_N = numbered([s for s in MLP_ORDER if s[0][0] != "T"], lambda s: T)
LN_AT, LN_N = numbered([("proj", 0), ("proj", 1), ("fc", 0), ("T2", 0), ("fc", 1), ("T2", 1), ("T3", 0), ("T3", 1)],
                       lambda s: T // 2)


def t_bank(n):
    return BANK_T if T_AT["o", 0] <= n < T_AT["T1", 0] else BANK_PV + n % 2


def t_before(n):
    return max([m for m in range(n) if t_bank(m) == t_bank(n)], default=-1)


def build(nc, x, cond, mask, qkv_w, proj_w, proj_b, fc1_w, fc1_b, fc2_w, fc2_b, ada1_w, ada1_b, ada2_w, ada2_b,
          adb_w, adb_b, ssm_w1, ssm_b1, ssm_w2, ssm_b2, ff_w1, ff_b1, ff_w2, ff_b2, out):
    ctx = ExitStack()
    with ctx:
        ctx.enter_context(nc.allow_non_contiguous_dma(reason="small vectors spread over partitions"))

        def sb(name, shape, dt=F32):
            return ctx.enter_context(nc.sbuf_tensor(name, shape, dt))

        def sem(name):
            return ctx.enter_context(nc.semaphore(name))

        q_dram = nc.dram_tensor("q_dram", [2, C, N], F32, kind="Internal").ap()
        k_dram = nc.dram_tensor("k_dram", [2, C, N], F32, kind="Internal").ap()
        mod_dram = nc.dram_tensor("mod_dram", [B, 12, C], F32, kind="Internal").ap()
        neg_dram = nc.dram_tensor("neg_dram", [B, N], F32, kind="Internal").ap()

        weights = {}
        for name, rows, cols in (("qkv", C, 3 * C), ("proj", C, C), ("fc1", C, FF0), ("fc2", FF0, C),
                                 ("ssm1", C, C), ("ssm2", C, C), ("ff1", C, FF1), ("ff2", FF1, C)):
            weights[name] = [sb(f"{name}_{part}", [P, rows // P, cols], F32R) for part in ("hi", "lo")]
        x_tok = sb("x_tok", [P, NCH * T, C])
        actT = {s: [sb(f"act{s}_{part}", [P, KC, CH], F32R) for part in ("hi", "lo")] for s in "ABC"}
        qa = sb("qa", [ROWS_S2, QSLOTS, HG, CH], F32R)
        ka = sb("ka", [ROWS_S2, H * FAST.keys], F32R)
        v_sb = sb("v_sb", [P, N // P, H, VW])
        probs = sb("probs", [P, 2, HG, CH])
        o_sb = sb("o_sb", [P, 2, CH])
        o_tok = sb("o_tok", [P, T, C])
        hid = sb("hid", [P, HSLOTS, 2, CH], F32R)
        stage = sb("stage", [P, 6 * C])
        up_raw = sb("up_raw", [P, 6 * C])
        vec = sb("vec", [P, 10, C])
        cols = sb("cols", [P, KC, 4, B])
        ident = sb("ident", [P, P])
        mpart = sb("mpart", [P, 2, HG, T, 2])
        mmax = sb("mmax", [P, 2, HG * T])
        mhl = sb("mhl", [P, 2, 2 * HG * T], F32R)
        m_rows = sb("m_rows", [2 * HG * T, 2, P], F32R)
        rden = sb("rden", [P, T, HG])
        mask_rows = sb("mask_rows", [B * N // P, P], U8)
        mask_neg = sb("mask_neg", [B * N // P, P], F32R)
        mask_col = sb("mask_col", [P, B * N // P])
        flags = sb("flags", [1, 2 * B], I32)
        condT = sb("condT", [P, KC, B])
        silu0 = sb("silu0", [P, KC, B])
        silu1 = sb("silu1", [P, KC, B])
        ada1b = sb("ada1b", [P, KC])
        fc1b = sb("fc1b", [P, FF0 // P])
        upb = sb("upb", [P, (C + FF1) // P])
        upb_mod = sb("upb_mod", [P, (C + FF1) // P, B])
        stats = sb("stats", [P, 2, 6])
        mv = sb("mv", [P, 4, 2, 2])
        veps = sb("veps", [P, 4, 2])
        rstd = sb("rstd", [P, 4, 2])
        mhalf = sb("mhalf", [P, 2])
        eps0 = sb("eps0", [P, 2])
        eps1 = sb("eps1", [P, 2])
        scratch = probs[:, :, :, :].rearrange("p a h n -> p (a h n)")
        gelu_out = scratch[:, 0:2 * CH].rearrange("p (s n) -> p s n", s=2)
        a_tok = [scratch[:, 2 * CH + c * T * C:2 * CH + (c + 1) * T * C].rearrange("p (t c) -> p t c", t=T) for c in range(NCH)]
        qkv_raw = v_sb[:, :, :, :].rearrange("p a h n -> p (a h n)")[:, 0:6 * C].rearrange("p (k n) -> p k n", k=KC)
        ada_raw = scratch[:, 0:12 * C].rearrange("p (k n) -> p k n", k=KC)
        mask_f = scratch[0:B * N // P, 12 * C:12 * C + P]
        mask_line = scratch[0:1, 13 * C:15 * C].bitcast(U8).rearrange("o (b n) -> o b n", b=B)
        ada1_raw = o_tok[:, :, :].rearrange("p t c -> p (t c)")[:, 0:2 * C].rearrange("p (k n) -> p k n", k=KC)
        ada_row = vec[0:B, 0:8, :]
        bias_row = up_raw[0:B, :].rearrange("b (r c) -> b r c", c=C)
        down_b_row = o_sb[0:B, :, 0:C]

        ps = ctx.enter_context(nc.psum_tensor("ps", [P, 8, 512], F32))

        s_x = [sem(f"x_loaded{c}") for c in range(NCH)]
        s_mask, s_qkv_raw, s_small, s_cond = sem("mask_loaded"), sem("qkv_loaded"), sem("small_loaded"), sem("cond_loaded")
        s_ada_raw = [sem(f"ada_loaded{n}") for n in range(2)]
        s_bias_row = [sem(f"bias_row_loaded{n}") for n in range(2)]
        s_stage = [sem(f"stage_loaded{n}") for n in range(2)]
        s_up_raw = sem("up_weights_loaded")
        s_ident, s_const, s_dset = sem("ident_made"), sem("consts_made"), sem("dve_setup")
        s_maskT, s_flags = sem("mask_transposed"), sem("flags_made")
        s_qkv_hi, s_qkv_lo = sem("qkv_hi_made"), sem("qkv_lo_made")
        s_ada_mm, s_silu, s_ada_row, s_ones = sem("ada_mm"), sem("silu_made"), sem("ada_rows_made"), sem("ones_packed")
        s_mod_out = [sem(f"mod_stored{n}") for n in range(2)]
        s_vec, s_cols, s_upb = sem("vec_loaded"), sem("cols_loaded"), sem("up_bias_made")
        s_neg_out, s_split, s_poolw = sem("neg_stored"), sem("weights_split"), sem("pool_weights")
        s_alone = sem("waits_alone")
        s_t_mm, s_t_hi, s_t_lo = sem("transposed"), sem("transposed_hi"), sem("transposed_lo")
        s_q_mm, s_q_hi, s_q_lo = sem("q_mm"), sem("q_hi"), sem("q_lo")
        s_q_out = [sem(f"q_stored{c}") for c in range(NCH)]
        s_tok_mm, s_tok_free = sem("tok_mm"), sem("tok_evacuated")
        s_up_mm, s_gelu, s_h_hi, s_h_lo, s_h_used = sem("up_mm"), sem("gelu_made"), sem("h_hi"), sem("h_lo"), sem("h_used")
        s_bn, s_aggr, s_eps, s_rstd = sem("bn_stats"), sem("bn_aggr"), sem("eps_added"), sem("rstd_made")
        s_cen, s_norm = sem("centred"), sem("normalised")
        s_res = sem("residual_shifted")
        s_wmod = sem("weights_modulated")
        s_out = [sem(f"out_stored{c}") for c in range(NCH)]

        class PathSems:
            def __init__(self, p):
                self.k_mm, self.k_hi, self.k_lo = [sem(f"{p.name}_k_{w}") for w in ("mm", "hi", "lo")]
                self.k_out, self.ka = sem(f"{p.name}_k_stored"), sem(f"{p.name}_keys_packed")
                self.v_mm, self.v = sem(f"{p.name}_v_mm"), sem(f"{p.name}_v_made")
                self.qa = [sem(f"{p.name}_queries_packed{n}") for n in range(QSLOTS)]
                self.m = [sem(f"{p.name}_max_packed{n}") for n in range(QSLOTS)]
                self.s1, self.max = sem(f"{p.name}_s1_mm"), sem(f"{p.name}_max")
                self.fold, self.neg, self.mT, self.mT_sb = [sem(f"{p.name}_m_{w}") for w in ("fold", "neg", "T", "T_copied")]
                self.s2, self.exp, self.pv = sem(f"{p.name}_s2_mm"), sem(f"{p.name}_exp"), sem(f"{p.name}_pv")
                self.o_sb, self.oT, self.rden, self.o = [sem(f"{p.name}_o_{w}") for w in ("copied", "T", "rden", "made")]

        sems = {p.name: PathSems(p) for p in (FAST, FULL)}
        block = ctx.enter_context(nc.Block())

        def slot_uses(u):
            return u // QSLOTS + 1

        def slot_total(u):
            return len([w for w in range(UNITS) if w % QSLOTS == u % QSLOTS])

        def qk_buf(m):
            m %= QK_BUFS
            return [actT["C"][part][:, m, :] if m < 2 else hid[:, m - 2, part, :] for part in range(2)]

        def x_tile(act, part, n0, n):
            c, at = n0 // CH, n0 % CH
            return [actT["AB"[c]][part][:, k, at:at + n] for k in range(KC)]

        def alone(e):
            e.sem_inc(s_alone, 1)

        def wait_before(e, b, semaphore, each):
            assert B == 2
            with e.If(b != 0):
                e.wait_ge(semaphore, each)
                e.nop()

        def batches(e, body):
            e.wait_ge(s_flags, 2)
            full0 = e.value_load(flags[0:1, 0:1], min_val=0, max_val=1)
            fast0 = e.value_load(flags[0:1, B:B + 1], min_val=0, max_val=1)
            with e.Fori(0, B) as b:
                body(b, {"full": b * full0, "fast": b * fast0})

        def by_path(e, b, seen, run):
            full = e.value_load(flags[0:1, bass.ds(b, 1)], min_val=0, max_val=1)
            with e.If(full != 0):
                run(FULL, sems["full"], seen["full"])
            with e.Else():
                run(FAST, sems["fast"], seen["fast"])

        @block.sync
        def _(sp):
            def load_x(b, c):
                sp.dma_start(x_tok[:, c * T:(c + 1) * T, :],
                             x[bass.ds(b, 1), c * CH:(c + 1) * CH, :].rearrange("o (t p) f -> p (o t) f", p=P)).then_inc(s_x[c], 16)

            def load_weights(dst, src, signal):
                sp.dma_start(dst, src.rearrange("(k p) n -> p k n", p=P)).then_inc(signal, 16)

            def load_bias(layer, src):
                sp.dma_start(bias_row, src.rearrange("(o r c) -> o r c", o=1, c=C).broadcast_to([B, 6, C]))\
                    .then_inc(s_bias_row[layer], 16)

            sp.dma_start(mask_line, mask.rearrange("(o b) n -> o b n", o=1)).then_inc(s_mask, 16)
            sp.dma_start(mask_rows[:, :], mask.rearrange("b (t p) -> (b t) p", p=P)).then_inc(s_mask, 16)
            for bb in range(B):
                sp.dma_start(condT[:, :, bb], cond[bb, :].rearrange("(k p) -> p k", p=P)).then_inc(s_cond, 16)
            sp.dma_start(ada1b[:, :], ada1_b.rearrange("(k p) -> p k", p=P)).then_inc(s_cond, 16)
            load_weights(ada1_raw, ada1_w, s_cond)
            load_weights(qkv_raw, qkv_w, s_qkv_raw)
            load_x(0, 0)
            load_x(0, 1)
            load_weights(ada_raw, ada2_w, s_ada_raw[0])
            load_bias(0, ada2_b)
            for r, b_dram in enumerate((ssm_b2, ff_b2)):
                sp.dma_start(down_b_row[:, r, :], b_dram.rearrange("(o c) -> o c", o=1).broadcast_to([B, C]))\
                    .then_inc(s_small, 16)
            sp.dma_start(fc1b[:, :], fc1_b.rearrange("(k p) -> p k", p=P)).then_inc(s_small, 16)
            sp.dma_start(upb[:, 0:C // P], ssm_b1.rearrange("(k p) -> p k", p=P)).then_inc(s_small, 16)
            sp.dma_start(upb[:, C // P:], ff_b1.rearrange("(k p) -> p k", p=P)).then_inc(s_small, 16)
            for r, b_dram in enumerate((proj_b, fc2_b)):
                sp.dma_start(vec[:, 8 + r, :], b_dram.rearrange("(o c) -> o c", o=1).broadcast_to([P, C]))\
                    .then_inc(s_small, 16)
            sp.wait_ge(s_dset, 2)
            sp.dma_start(neg_dram.rearrange("b (t p) -> (b t) p", p=P), mask_neg[:, :].bitcast(F32)).then_inc(s_neg_out, 16)
            sp.wait_ge(s_const, 5)
            ones = qa[ROW_MASK:ROW_MASK + 2, :, :, :].rearrange("r s h n -> r (s h n)")
            sp.dma_start(ka[ROW_MAX:ROW_MAX + 2, :].bitcast(F32), ones[:, 0:H * FAST.keys].bitcast(F32)).then_inc(s_ones, 16)
            sp.wait_ge(s_neg_out, 16)
            sp.wait_ge(s_ones, 16)

            def body(b, seen):
                assert B == 2
                with sp.If(b != 0):
                    sp.wait_ge(s_tok_free, (TOK_AT["ff", 1] + T) // 2)
                    load_x(b, 1)

                def run(p, s, seen):
                    def load_rows(dram, part, heads, n0, n, dst, signal):
                        sp.dma_start(dst.bitcast(F32), dram[part, heads.start * D:heads.stop * D, n0:n0 + n]
                                     .rearrange("(h d) n -> d h n", d=D)).then_inc(signal, 16)

                    for step in p.order():
                        if step[0] == "k":
                            n = step[1]
                            fc, blk = divmod(n, p.blocks)
                            at = N - p.keys + blk * p.block
                            sp.wait_ge(s.k_lo, seen * p.k_tiles + n + 1)
                            for part in range(2):
                                sp.dma_start(k_dram[part, fc * P:(fc + 1) * P, at:at + p.block],
                                             qk_buf(p.projected().index(step))[part][:, 0:p.block].bitcast(F32)).then_inc(s.k_out, 16)
                        elif step[0] == "q":
                            n = step[1]
                            c, fc = divmod(n, KC)
                            sp.wait_ge(s_q_lo, b * Q_N + n + 1)
                            for part in range(2):
                                sp.dma_start(q_dram[part, fc * P:(fc + 1) * P, c * CH:(c + 1) * CH],
                                             qk_buf(p.projected().index(step))[part].bitcast(F32)).then_inc(s_q_out[c], 16)
                        elif step[0] == "adb":
                            with sp.If(b == 0):
                                sp.wait_ge(s_ada_mm, 2)
                                load_weights(ada_raw, adb_w, s_ada_raw[1])
                                sp.wait_ge(s_ada_row, 5)
                                for row, at in ((H1, 0), (H2, 3)):
                                    sp.dma_start(mod_dram[:, row:row + 2, :], ada_row[:, at:at + 2, :]).then_inc(s_mod_out[0], 16)
                                load_bias(1, adb_b)
                        elif step[0] == "ka":
                            u = step[1]
                            if u == 0:
                                sp.wait_ge(s.k_out, seen * (32 * KC * p.blocks) + 32 * KC * p.blocks)
                            else:
                                sp.wait_ge(s.s2, seen * (UNITS * p.n2) + u * p.n2)
                            alone(sp)
                            first = (u % NG) * HG if p.heads == HG else 0
                            heads = range(first, first + p.heads)
                            kav = ka[:, :].rearrange("r (h n) -> r h n", h=p.heads)
                            for row, part in ((ROW_A, 0), (ROW_B, 1), (ROW_C, 0)):
                                load_rows(k_dram, part, heads, N - p.keys, p.keys, kav[row:row + D, :, :], s.ka)
                            sp.dma_start(kav[ROW_MASK:ROW_MASK + 1, :, :].bitcast(F32),
                                         neg_dram[bass.ds(b, 1), N - p.keys:N].rearrange("(o i) n -> o i n", i=1)
                                         .broadcast_to([1, p.heads, p.keys])).then_inc(s.ka, 16)
                        elif step[0] == "qa":
                            u = step[1]
                            c, g, slot = u // NG, u % NG, u % QSLOTS
                            if u % NG == 0 or u == 0:
                                sp.wait_ge(s_q_out[c], b * (32 * KC) + 32 * KC)
                                alone(sp)
                            if u >= QSLOTS:
                                sp.wait_ge(s.s2, seen * (UNITS * p.n2) + (u - QSLOTS + 1) * p.n2)
                            for row, part in ((ROW_A, 0), (ROW_B, 0), (ROW_C, 1)):
                                load_rows(q_dram, part, range(g * HG, (g + 1) * HG), c * CH, CH,
                                          qa[row:row + D, slot, :, :], s.qa[slot])
                        elif step[0] == "mT":
                            u = step[1]
                            slot = u % QSLOTS
                            sp.wait_ge(s.mT_sb, seen * UNITS + u + 1)
                            for part in range(2):
                                sp.dma_start(qa[ROW_MAX + part:ROW_MAX + part + 1, slot, :, :].bitcast(F32)
                                             .rearrange("r h (t q) -> r (h t) q", q=P),
                                             m_rows[part * HG * T:(part + 1) * HG * T, u % 2, :].bitcast(F32)).then_inc(s.m[slot], 16)

                by_path(sp, b, seen, run)
                for c in range(NCH):
                    sp.wait_ge(s_tok_free, b * (TOK_N // 2) + (TOK_AT["ff", c] + T) // 2)
                    alone(sp)
                    sp.dma_start(out[bass.ds(b, 1), c * CH:(c + 1) * CH, :].rearrange("o (t p) f -> p (o t) f", p=P),
                                 o_tok[:, :, :] if c == 0 else a_tok[1]).then_inc(s_out[c], 16)
                    if c == 0:
                        with sp.If(b == 0):
                            load_x(1, 0)

            batches(sp, body)
            for c in range(NCH):
                sp.wait_ge(s_out[c], 16 * B)

        @block.gpsimd
        def _(pool):
            pool.memset(ident[:, :], 0.0).then_inc(s_ident, 1)
            pool.wait_ge(s_ident, 1)
            pool.affine_select(out=ident[:, :], in_=ident[:, :], compare_op=ALU.not_equal, fill=1.0, base=0,
                               pattern=[[-1, P]], channel_multiplier=1).then_inc(s_ident, 1)
            for tile, value in ((mhalf, -0.5), (eps0, EPS0), (eps1, EPS1)):
                pool.memset(tile[:, :], value).then_inc(s_const, 1)

            def split(src, hi, lo, value, signal, count):
                pool.tensor_copy(hi, src).then_inc(signal, 1)
                pool.wait_ge(signal, value + 1)
                return pool.tensor_tensor(lo, src, hi.bitcast(F32), ALU.subtract).then_inc(signal, 1)

            def staged(n):
                return stage[:, 0:n]

            pool.memset(ka[0:ROW_MAX, :].bitcast(F32), 0.0).then_inc(s_const, 1)
            pool.memset(qa[0:ROW_MAX, :, :, :].bitcast(F32), 1.0).then_inc(s_const, 1)

            pieces = []
            for name, dram in (("proj", proj_w), ("fc1", fc1_w), ("fc2", fc2_w)):
                chunks, n = weights[name][0].shape[1], weights[name][0].shape[2]
                width = min(n, 2 * C)
                pieces += [(name, dram, k, min(2 * C // width, chunks - k), at, width)
                           for k in range(0, chunks, 2 * C // width) for at in range(0, n, width)]

            def piece_raw(i):
                _, _, _, m, _, width = pieces[i]
                return stage[:, (i % 2) * 3 * C:(i % 2) * 3 * C + m * width].rearrange("p (k n) -> p k n", n=width)

            def load_piece(i):
                _, dram, k, m, at, width = pieces[i]
                pool.dma_start(piece_raw(i), dram.rearrange("(k p) n -> p k n", p=P)[:, k:k + m, at:at + width])\
                    .then_inc(s_stage[i % 2], 16)

            load_piece(0)
            for i, (name, dram, k, m, at, width) in enumerate(pieces):
                if i:
                    pool.wait_ge(s_split, 2 * i)
                if i + 1 < len(pieces):
                    load_piece(i + 1)
                pool.wait_ge(s_stage[i % 2], 16 * (i // 2 + 1))
                split(piece_raw(i), weights[name][0][:, k:k + m, at:at + width], weights[name][1][:, k:k + m, at:at + width],
                      2 * i, s_split, 2)
            assert 2 * len(pieces) == SPLITS
            staged = [(len(pieces) + 1 - half) // 2 for half in range(2)]
            pool.wait_ge(s_split, 2 * len(pieces))

            def first_rows():
                pool.wait_ge(s_ada_row, 10)
                for row, at, n in ((GS, 2, 1), (GF, 5, 3), (SH_S, 0, 2), (SH_F, 3, 2)):
                    pool.dma_start(mod_dram[:, row:row + n, :], ada_row[:, at:at + n, :]).then_inc(s_mod_out[1], 16)
                pool.dma_start(up_raw[:, 0:2 * C].rearrange("p (k n) -> p k n", k=KC),
                               ssm_w1.rearrange("(k p) n -> p k n", p=P)).then_inc(s_up_raw, 16)
                pool.dma_start(up_raw[:, 2 * C:6 * C].rearrange("p (k n) -> p k n", k=KC),
                               ff_w1.rearrange("(k p) n -> p k n", p=P)).then_inc(s_up_raw, 16)
                pool.wait_ge(s_mod_out[0], 32)
                pool.wait_ge(s_mod_out[1], 64)
                for k in range(KC):
                    for bb in range(B):
                        pool.dma_start(cols[:, k, :, bb], mod_dram[bb, SH_S:SC_F + 1, k * P:(k + 1) * P].rearrange("r p -> p r"))\
                            .then_inc(s_cols, 16)

            def body(b, seen):
                with pool.If(b == 0):
                    first_rows()
                wait_before(pool, b, s_norm, 2 * LN_N)
                wait_before(pool, b, s_wmod, 4)
                wait_before(pool, b, s_res, 8)
                pool.dma_start(vec[:, 0:8, :], mod_dram[bass.ds(b, 1), 0:8, :].broadcast_to([P, 8, C])).then_inc(s_vec, 16)
                mods = (("ssm1", ssm_w1, 1, None), ("ff1", ff_w1, 3, None), ("ssm2", ssm_w2, None, GS), ("ff2", ff_w2, None, GF))

                def mod_raw(i):
                    chunks, n = weights[mods[i][0]][0].shape[1:]
                    at = 2 * C * (i % 2)
                    return stage[:, at:at + chunks * n].rearrange("p (k n) -> p k n", n=n)

                def load_mod(i):
                    pool.dma_start(mod_raw(i), mods[i][1].rearrange("(k p) n -> p k n", p=P)).then_inc(s_stage[i % 2], 16)

                load_mod(0)
                load_mod(1)
                wait_before(pool, b, s_tok_mm, TOK_N)
                pool.wait_ge(s_vec, b * 16 + 16)
                alone(pool)
                pool.wait_ge(s_cols, 16 * KC * B)
                at = 0
                for i, (name, dram, col, row) in enumerate(mods):
                    chunks, n = weights[name][0].shape[1], weights[name][0].shape[2]
                    raw = mod_raw(i)
                    pool.wait_ge(s_stage[i % 2], b * 32 + 16 * (staged[i % 2] + i // 2 + 1))
                    factor = [cols[:, k, col, bass.ds(b, 1)].broadcast_to([P, n]) if row is None else vec[:, row, :]
                              for k in range(chunks)]
                    for k in range(chunks):
                        pool.tensor_tensor(weights[name][0][:, k, :], raw[:, k, :], factor[k], ALU.mult).then_inc(s_poolw, 1)
                    at += chunks
                    pool.wait_ge(s_poolw, b * 20 + at)
                    alone(pool)
                    for k in range(chunks):
                        pool.tensor_tensor(raw[:, k, :], raw[:, k, :], factor[k], ALU.mult).then_inc(s_poolw, 1)
                    at += chunks
                    pool.wait_ge(s_poolw, b * 20 + at)
                    pool.tensor_tensor(weights[name][1][:, :, :], raw, weights[name][0][:, :, :].bitcast(F32), ALU.subtract)\
                        .then_inc(s_wmod, 1)
                    if i + 2 < len(mods):
                        pool.wait_ge(s_wmod, b * 4 + i + 1)
                        alone(pool)
                        load_mod(i + 2)

                def shift(n, c, row):
                    xc = x_tok[:, c * T:(c + 1) * T, :]
                    pool.tensor_tensor(xc, xc, vec[:, row, :].rearrange("p (o c) -> p o c", o=1).broadcast_to([P, T, C]),
                                       ALU.add).then_inc(s_res, 1)

                def inverse_std(step, eps):
                    for pair in range(2):
                        n = LN_AT[step] + pair
                        pool.wait_ge(s_aggr, b * (2 * LN_N) + 2 * (n + 1))
                        pool.tensor_tensor(veps[:, n % 4, :], mv[:, n % 4, :, 1], eps, ALU.add).then_inc(s_eps, 1)
                        pool.wait_ge(s_eps, b * LN_N + n + 1)
                        pool.tensor_tensor(rstd[:, n % 4, :], veps[:, n % 4, :], mhalf[:, :], ALU.pow).then_inc(s_rstd, 1)

                def low_part(step, j):
                    n = H_AT[step] + j
                    pool.wait_ge(s_h_hi, b * H_N + n + 1)
                    pool.tensor_tensor(hid[:, n % HSLOTS, 1, :], gelu_out[:, n % 2, :], hid[:, n % HSLOTS, 0, :].bitcast(F32),
                                       ALU.subtract).then_inc(s_h_lo, 1)

                for c in range(NCH):
                    pool.wait_ge(s_t_mm, b * T_N + T_AT["x", c] + 2)
                    shift(c, c, 0)
                pool.wait_ge(s_const, 3)
                inverse_std(("proj", 0), eps0[:, :])
                inverse_std(("proj", 1), eps0[:, :])
                pool.wait_ge(s_t_mm, b * T_N + T_AT["T1", 0] + 2)
                shift(2, 0, 2)
                for j in range(HIDDEN["fc"]):
                    low_part(("fc", 0), j)
                pool.wait_ge(s_t_mm, b * T_N + T_AT["T1", 1] + 2)
                shift(3, 1, 2)
                low_part(("fc", 1), 0)
                inverse_std(("fc", 0), eps0[:, :])
                for j in (1, 2):
                    low_part(("fc", 1), j)
                inverse_std(("T2", 0), eps1[:, :])
                for j in range(3, HIDDEN["fc"]):
                    low_part(("fc", 1), j)
                pool.wait_ge(s_norm, b * (2 * LN_N) + 2 * (LN_AT["T2", 0] + 2))
                shift(4, 0, 6)
                inverse_std(("fc", 1), eps0[:, :])
                for j in range(HIDDEN["ssm"]):
                    low_part(("ssm", 0), j)
                inverse_std(("T2", 1), eps1[:, :])
                pool.wait_ge(s_norm, b * (2 * LN_N) + 2 * (LN_AT["T2", 1] + 2))
                shift(5, 1, 6)
                inverse_std(("T3", 0), eps1[:, :])
                for j in range(HIDDEN["ssm"]):
                    low_part(("ssm", 1), j)
                pool.wait_ge(s_norm, b * (2 * LN_N) + 2 * (LN_AT["T3", 0] + 2))
                shift(6, 0, 7)
                inverse_std(("T3", 1), eps1[:, :])
                for j in range(HIDDEN["ff"]):
                    low_part(("ff", 0), j)
                pool.wait_ge(s_norm, b * (2 * LN_N) + 2 * (LN_AT["T3", 1] + 2))
                shift(7, 1, 7)
                for j in range(HIDDEN["ff"]):
                    low_part(("ff", 1), j)

            with pool.Fori(0, B) as b:
                body(b, None)

        @block.scalar
        def _(act):
            act.wait_ge(s_cond, 16 * (B + 2))
            act.activation(silu1[:, :, :], condT[:, :, :], ACT.Silu).then_inc(s_silu, 1)
            act.wait_ge(s_ada_mm, 1)
            for f in range(KC):
                act.activation(silu0[:, f, :], ps[:, BANK_FEAT, f * B:(f + 1) * B], ACT.Silu, bias=ada1b[:, f:f + 1])\
                    .then_inc(s_silu, 1)
            act.wait_ge(s_qkv_raw, 16)
            act.activation(weights["qkv"][0][:, :, :], qkv_raw, ACT.Identity).then_inc(s_qkv_hi, 1)

            def body(b, seen):
                def high(step, slot):
                    for pair in range(T // 2):
                        n = T_AT[step] + pair
                        act.wait_ge(s_t_mm, b * T_N + n + 1)
                        act.activation(actT[slot][0][:, :, pair * C:(pair + 1) * C],
                                       ps[:, t_bank(n), :].rearrange("p (k n) -> p k n", k=KC), ACT.Identity)\
                           .then_inc(s_t_hi, 1)

                wait_before(act, b, s_tok_mm, TOK_N)

                def run(p, s, seen):
                    def buffer_stored(m):
                        if m >= QK_BUFS and p.projected()[m - QK_BUFS][0] == "k":
                            act.wait_ge(s.k_out, seen * (32 * p.k_tiles) + 32 * p.k_tiles)
                        elif m >= QK_BUFS:
                            act.wait_ge(s_q_out[0], b * (32 * KC) + 32 * KC)

                    for step in p.order():
                        if step[0] == "k":
                            n = step[1]
                            m = p.projected().index(step)
                            act.wait_ge(s.k_mm, seen * p.k_tiles + n + 1)
                            buffer_stored(m)
                            act.activation(qk_buf(m)[0][:, 0:p.block], ps[:, BANK_FEAT + m % 2, 0:p.block], ACT.Identity)\
                               .then_inc(s.k_hi, 1)
                        elif step[0] == "x":
                            high(step, "AB"[step[1]])
                        elif step[0] == "q":
                            n = step[1]
                            m = p.projected().index(step)
                            act.wait_ge(s_q_mm, b * Q_N + n + 1)
                            buffer_stored(m)
                            act.activation(qk_buf(m)[0], ps[:, BANK_FEAT + m % 2, :], ACT.Identity).then_inc(s_q_hi, 1)
                        elif step[0] == "mT":
                            u = step[1]
                            act.wait_ge(s.mT, seen * UNITS + u + 1)
                            if u >= 2:
                                act.wait_ge(s.m[(u - 2) % QSLOTS], seen * (32 * slot_total(u - 2)) + 32 * slot_uses(u - 2))
                            act.activation(m_rows[:, u % 2, :], ps[0:2 * HG * T, BANK_T, 0:P], ACT.Identity).then_inc(s.mT_sb, 1)
                        elif step[0] == "s2":
                            _, u, kt, hp = step
                            n, v = u * p.n2 + 2 * kt + hp, u * p.kt + kt
                            act.wait_ge(s.s2, seen * (UNITS * p.n2) + n + 1)
                            if v >= 2:
                                act.wait_ge(s.pv, seen * (UNITS * p.kt) + v - 1)
                            act.activation(probs[:, kt % 2, 2 * hp:2 * hp + 2, :], ps[:, 2 * hp:2 * hp + 2, :], ACT.Exp,
                                           scale=SCALE).then_inc(s.exp, 1)
                        elif step[0] == "o":
                            u = step[1]
                            act.wait_ge(s.pv, seen * (UNITS * p.kt) + (u + 1) * p.kt)
                            if u == 0:
                                act.wait_ge(s_ada_row, 10)
                            if u >= 2:
                                act.wait_ge(s.oT, seen * UNITS + u - 1)
                            act.activation(o_sb[:, u % 2, :], ps[:, BANK_PV, :], ACT.Identity).then_inc(s.o_sb, 1)
                        elif step[0] == "attnT":
                            high(("o", step[1]), "AB"[step[1]])

                by_path(act, b, seen, run)
                act.wait_ge(s_upb, 2)
                act.wait_ge(s_small, 16 * 7)
                bias = {"fc": lambda j: fc1b[:, j:j + 1], "ssm": lambda j: upb_mod[:, j, bass.ds(b, 1)],
                        "ff": lambda j: upb_mod[:, C // P + j, bass.ds(b, 1)]}
                for step in MLP_ORDER:
                    if step[0][0] == "T":
                        high(step, "CA"[step[1]])
                    elif step[0] in HIDDEN:
                        for j in range(HIDDEN[step[0]]):
                            n = H_AT[step] + j
                            act.wait_ge(s_up_mm, b * H_N + n + 1)
                            if n >= 2:
                                act.wait_ge(s_h_lo, b * H_N + n - 1)
                            alone(act)
                            act.activation(gelu_out[:, n % 2, :], ps[:, BANK_FEAT + n % 2, :],
                                           ACT.Gelu_apprx_tanh if step[0] == "ff" else ACT.Gelu, bias=bias[step[0]](j))\
                               .then_inc(s_gelu, 1)
                            act.wait_ge(s_gelu, b * H_N + n + 1)
                            if n >= HSLOTS:
                                act.wait_ge(s_h_used, b * H_N + n - HSLOTS + 1)
                            act.activation(hid[:, n % HSLOTS, 0, :], gelu_out[:, n % 2, :], ACT.Identity).then_inc(s_h_hi, 1)

            batches(act, body)

        @block.vector
        def _(dve):
            dve.wait_ge(s_mask, 32)
            dve.tensor_copy(mask_f, mask_rows[:, :]).then_inc(s_dset, 1)
            dve.wait_ge(s_dset, 1)
            dve.tensor_scalar(mask_neg[:, :], mask_f, 1.0, -MASKED, ALU.subtract, ALU.mult).then_inc(s_dset, 1)
            dve.tensor_reduce(flags[0:1, 0:B], mask_line[:, :, 0:N - FAST.keys], axis=AX.X, op=ALU.max).then_inc(s_flags, 1)
            dve.wait_ge(s_flags, 1)
            dve.tensor_scalar(flags[0:1, B:2 * B], flags[0:1, 0:B], -1.0, 1.0, ALU.mult, ALU.add).then_inc(s_flags, 1)
            dve.wait_ge(s_maskT, 1)
            dve.tensor_copy(mask_col[:, :], ps[:, BANK_T, 0:B * N // P]).then_inc(s_dset, 1)
            dve.memset(ps[:, BANK_PV, :], 0.0).then_inc(s_dset, 1)
            dve.wait_ge(s_qkv_hi, 1)
            dve.tensor_tensor(weights["qkv"][1][:, :, :], qkv_raw, weights["qkv"][0][:, :, :].bitcast(F32), ALU.subtract)\
               .then_inc(s_qkv_lo, 1)

            def modulation_rows(layer):
                base = 5 * layer
                bank = ADA_BANK[layer]
                dve.wait_ge(s_ada_mm, 2 + layer)
                dve.wait_ge(s_bias_row[layer], 16)
                if layer:
                    dve.wait_ge(s_mod_out[0], 32)
                dve.tensor_tensor(ada_row[:, 0:6, :], ps[0:B, bank:bank + 3, :].rearrange("b a (r c) -> b (a r) c", c=C),
                                  bias_row, ALU.add).then_inc(s_ada_row, 1)
                dve.wait_ge(s_ada_row, base + 1)
                if layer == 0:
                    for i, half in enumerate((0, 3)):
                        shift, scale, gate = [ada_row[:, half + r, :] for r in range(3)]
                        dve.tensor_tensor(shift, shift, gate, ALU.mult).then_inc(s_ada_row, 1)
                        dve.scalar_tensor_tensor(out=scale, in0=scale, scalar=1.0, in1=gate, op0=ALU.add, op1=ALU.mult)\
                           .then_inc(s_ada_row, 1)
                else:
                    dve.wait_ge(s_small, 16 * 7)
                    for i, half in enumerate((0, 3)):
                        scale, gate = ada_row[:, half + 1, :], ada_row[:, half + 2, :]
                        dve.tensor_scalar(scale, scale, 1.0, None, ALU.add).then_inc(s_ada_row, 1)
                        dve.tensor_tensor(ada_row[:, 6 + i, :], gate, down_b_row[:, i, :], ALU.mult).then_inc(s_ada_row, 1)

            def body(b, seen):
                def low(step, slot):
                    for pair in range(T // 2):
                        n = T_AT[step] + pair
                        cs = slice(pair * C, (pair + 1) * C)
                        dve.wait_ge(s_t_hi, b * T_N + n + 1)
                        dve.tensor_tensor(actT[slot][1][:, :, cs], ps[:, t_bank(n), :].rearrange("p (k n) -> p k n", k=KC),
                                          actT[slot][0][:, :, cs].bitcast(F32), ALU.subtract).then_inc(s_t_lo, 1)


                def run(p, s, seen):
                    for step in p.order():
                        if step[0] == "k":
                            n = step[1]
                            m = p.projected().index(step)
                            hi, lo = [buf[:, 0:p.block] for buf in qk_buf(m)]
                            dve.wait_ge(s.k_hi, seen * p.k_tiles + n + 1)
                            dve.tensor_tensor(lo, ps[:, BANK_FEAT + m % 2, 0:p.block], hi.bitcast(F32), ALU.subtract)\
                               .then_inc(s.k_lo, 1)
                        elif step[0] == "x":
                            low(step, "AB"[step[1]])
                        elif step[0] == "q":
                            n = step[1]
                            m = p.projected().index(step)
                            hi, lo = qk_buf(m)
                            dve.wait_ge(s_q_hi, b * Q_N + n + 1)
                            dve.tensor_tensor(lo, ps[:, BANK_FEAT + m % 2, :], hi.bitcast(F32), ALU.subtract).then_inc(s_q_lo, 1)
                        elif step[0] == "rows":
                            with dve.If(b == 0):
                                modulation_rows(step[1])
                        elif step[0] == "upb":
                            with dve.If(b == 0):
                                dve.wait_ge(s_upb, 1)
                                dve.tensor_tensor(upb_mod[:, :, :], ps[:, BANK_FEAT, 0:6 * B].rearrange("p (f b) -> p f b", b=B),
                                                  upb[:, :].rearrange("p (f o) -> p f o", o=1).broadcast_to([P, 6, B]), ALU.add)\
                                   .then_inc(s_upb, 1)
                        elif step[0] == "v":
                            n = step[1]
                            at = (N - p.keys) // P + n
                            m = mask_col[:, bass.ds(b * (N // P) + at, 1)]
                            dve.wait_ge(s.v_mm, seen * p.kt + n + 1)
                            dve.tensor_scalar(v_sb[:, n, :, 0:D],
                                              ps[:, BANK_TOK + n % 4, 0:C].rearrange("p (h d) -> p h d", d=D),
                                              m, None, ALU.mult).then_inc(s.v, 1)
                            dve.tensor_copy(v_sb[:, n, :, D], m.broadcast_to([P, H])).then_inc(s.v, 1)
                        elif step[0] == "s1":
                            _, u, i = step
                            n = u * p.n1 + i
                            dve.wait_ge(s.s1, seen * (UNITS * p.n1) + n + 1)
                            bank = ps[:, BANK_TOK + 2 + n % 2, :]
                            if p is FAST:
                                h, tp = divmod(i, T // 2)
                                if i == 0 and u >= 2:
                                    dve.wait_ge(s.neg, seen * (2 * UNITS) + 2 * (u - 1))
                                dve.tensor_reduce(mmax[:, u % 2, h * T + 2 * tp:h * T + 2 * tp + 2],
                                                  bank.rearrange("p (t n) -> p t n", t=2), axis=AX.X, op=ALU.max).then_inc(s.max, 1)
                            else:
                                h, t, half = i // (2 * T), i // 2 % T, i % 2
                                dve.tensor_reduce(mpart[:, u % 2, h, t, half:half + 1], bank, axis=AX.X, op=ALU.max)\
                                   .then_inc(s.max, 1)
                        elif step[0] == "mneg":
                            u = step[1]
                            dve.wait_ge(s.max, seen * (UNITS * p.n1) + (u + 1) * p.n1)
                            if p is FULL:
                                dve.tensor_reduce(mmax[:, u % 2, :], mpart[:, u % 2, :, :, :].rearrange("p h t a -> p (h t) a"),
                                                  axis=AX.X, op=ALU.max).then_inc(s.fold, 1)
                                dve.wait_ge(s.fold, seen * UNITS + u + 1)
                            if u >= 2:
                                dve.wait_ge(s.mT, seen * UNITS + u - 1)
                            hi, lo = mhl[:, u % 2, 0:HG * T], mhl[:, u % 2, HG * T:2 * HG * T]
                            dve.tensor_scalar(hi, mmax[:, u % 2, :], -1.0, None, ALU.mult).then_inc(s.neg, 1)
                            dve.wait_ge(s.neg, seen * (2 * UNITS) + 2 * u + 1)
                            dve.scalar_tensor_tensor(out=lo, in0=mmax[:, u % 2, :], scalar=-1.0, in1=hi.bitcast(F32),
                                                     op0=ALU.mult, op1=ALU.subtract).then_inc(s.neg, 1)
                        elif step[0] == "oT":
                            u = step[1]
                            c, g = u // NG, u % NG
                            if u == 0:
                                alone(dve)
                                wait_before(dve, b, s_out[0], 16)
                            dve.wait_ge(s.oT, seen * UNITS + u + 1)
                            if c and g == 0:
                                dve.wait_ge(s_t_mm, b * T_N + T_AT["o", c - 1] + 2)
                            if u >= 1:
                                dve.wait_ge(s.o, seen * UNITS + u)
                            bank = ps[:, BANK_T, :].rearrange("p (t h d) -> p t h d", t=T, h=HG)
                            dve.reciprocal(rden[:, :, :], bank[:, :, :, D]).then_inc(s.rden, 1)
                            dve.wait_ge(s.rden, seen * UNITS + u + 1)
                            dve.tensor_tensor(o_tok[:, :, g * HG * D:(g + 1) * HG * D].rearrange("p t (h d) -> p t h d", d=D),
                                              bank[:, :, :, 0:D],
                                              rden[:, :, :].rearrange("p t (h o) -> p t h o", o=1).broadcast_to([P, T, HG, D]),
                                              ALU.mult).then_inc(s.o, 1)
                        elif step[0] == "attnT":
                            low(("o", step[1]), "AB"[step[1]])

                by_path(dve, b, seen, run)

                def statistics(n, tiles):
                    for t in range(2):
                        if n:
                            dve.wait_ge(s_aggr, b * (2 * LN_N) + 2 * (n - 1) + t + 1)
                        dve.bn_stats(stats[:, t, :], tiles[t]).then_inc(s_bn, 1)
                    for t in range(2):
                        dve.wait_ge(s_bn, b * (2 * LN_N) + 2 * n + t + 1)
                        alone(dve)
                        dve.bn_aggr(mv[:, n % 4, t, :], stats[:, t, :]).then_inc(s_aggr, 1)

                def ln_in(step, bias):
                    for pair in range(2):
                        tok, n = TOK_AT[step] + 2 * pair, LN_AT[step] + pair
                        dve.wait_ge(s_tok_mm, b * TOK_N + tok + 2)
                        a = a_tok[step[1]][:, 2 * pair:2 * pair + 2, :]
                        bank = BANK_TOK + tok % 4
                        dve.tensor_tensor(a, ps[:, bank:bank + 2, 0:C],
                                          vec[:, bias, :].rearrange("p (o c) -> p o c", o=1).broadcast_to([P, 2, C]), ALU.add)\
                           .then_inc(s_tok_free, 1)
                        dve.wait_ge(s_tok_free, b * (TOK_N // 2) + tok // 2 + 1)
                        statistics(n, [a[:, t, :] for t in range(2)])

                def ln_apply(step, gain):
                    for pair in range(2):
                        n = LN_AT[step] + pair
                        dve.wait_ge(s_aggr, b * (2 * LN_N) + 2 * (n + 1))
                        for t in range(2):
                            a = a_tok[step[1]][:, 2 * pair + t, :]
                            dve.scalar_tensor_tensor(out=a, in0=a, scalar=mv[:, n % 4, t, 0:1], in1=vec[:, gain, :],
                                                     op0=ALU.subtract, op1=ALU.mult).then_inc(s_cen, 1)
                    for pair in range(2):
                        n = LN_AT[step] + pair
                        dve.wait_ge(s_rstd, b * LN_N + n + 1)
                        for t in range(2):
                            a = a_tok[step[1]][:, 2 * pair + t, :]
                            xt = x_tok[:, step[1] * T + 2 * pair + t, :]
                            dve.wait_ge(s_cen, b * 16 + CEN_AT[step] + 2 * pair + t + 1)
                            dve.scalar_tensor_tensor(out=xt, in0=a, scalar=rstd[:, n % 4, t:t + 1], in1=xt,
                                                     op0=ALU.mult, op1=ALU.add).then_inc(s_norm, 1)

                def z_in(step, ready):
                    for pair in range(2):
                        ready(pair)
                        statistics(LN_AT[step] + pair, [x_tok[:, step[1] * T + 2 * pair + t, :] for t in range(2)])

                def z_apply(step):
                    for pair in range(2):
                        n = LN_AT[step] + pair
                        dve.wait_ge(s_rstd, b * LN_N + n + 1)
                        for t in range(2):
                            dve.tensor_scalar(a_tok[step[1]][:, 2 * pair + t, :], x_tok[:, step[1] * T + 2 * pair + t, :],
                                              mv[:, n % 4, t, 0:1], rstd[:, n % 4, t:t + 1], ALU.subtract, ALU.mult).then_inc(s_norm, 1)

                def add_residual(step, dst):
                    for pair in range(2):
                        tok = TOK_AT[step] + 2 * pair
                        ts = slice(2 * pair, 2 * pair + 2)
                        bank = BANK_TOK + tok % 4
                        dve.wait_ge(s_tok_mm, b * TOK_N + tok + 2)
                        dve.tensor_tensor(dst[:, ts, :], ps[:, bank:bank + 2, 0:C],
                                          x_tok[:, step[1] * T + 2 * pair:step[1] * T + 2 * pair + 2, :], ALU.add)\
                           .then_inc(s_tok_free, 1)

                def after_norm(step):
                    def ready(pair):
                        dve.wait_ge(s_norm, b * (2 * LN_N) + 2 * LN_AT[step] + 2 * pair + 2)
                    return ready

                def after_add(step):
                    def ready(pair):
                        dve.wait_ge(s_tok_free, b * (TOK_N // 2) + TOK_AT[step] // 2 + pair + 1)
                    return ready

                def res(n):
                    dve.wait_ge(s_res, b * 8 + n)

                def a_free(step):
                    dve.wait_ge(s_t_mm, b * T_N + T_AT[step] + 2)

                x_chunk = [x_tok[:, c * T:(c + 1) * T, :] for c in range(NCH)]
                wait_before(dve, b, s_out[1], 16)
                dve.wait_ge(s_vec, b * 16 + 16)
                ln_in(("proj", 0), 8)
                res(2)
                ln_apply(("proj", 0), 1)
                low(("T1", 0), "C")
                ln_in(("proj", 1), 8)
                ln_apply(("proj", 1), 1)
                low(("T1", 1), "A")
                dve.wait_ge(s_norm, b * (2 * LN_N) + 2 * (LN_AT["proj", 1] + 2))
                ln_in(("fc", 0), 9)
                res(4)
                ln_apply(("fc", 0), 3)
                z_in(("T2", 0), after_norm(("fc", 0)))
                z_apply(("T2", 0))
                low(("T2", 0), "C")
                ln_in(("fc", 1), 9)
                ln_apply(("fc", 1), 3)
                z_in(("T2", 1), after_norm(("fc", 1)))
                z_apply(("T2", 1))
                low(("T2", 1), "A")
                res(5)
                add_residual(("ssm", 0), x_chunk[0])
                z_in(("T3", 0), after_add(("ssm", 0)))
                z_apply(("T3", 0))
                low(("T3", 0), "C")
                res(6)
                add_residual(("ssm", 1), x_chunk[1])
                z_in(("T3", 1), after_add(("ssm", 1)))
                z_apply(("T3", 1))
                low(("T3", 1), "A")
                res(7)
                add_residual(("ff", 0), o_tok)
                res(8)
                add_residual(("ff", 1), a_tok[1])

            CEN_AT = {("proj", 0): 0, ("proj", 1): 4, ("fc", 0): 8, ("fc", 1): 12}
            batches(dve, body)

        @block.tensor
        def _(pe):
            def product(dst, left, right, start=True, stop=True):
                n = len(left[0])
                for k in range(n):
                    for i, (a, w) in enumerate(((0, 0), (0, 1), (1, 0))):
                        last = pe.matmul(dst, left[a][k], right[w][k], start=start and k == 0 and i == 0,
                                         stop=stop and k == n - 1 and i == 2)
                return last

            pe.wait_ge(s_ident, 2)
            pe.wait_ge(s_dset, 1)
            pe.transpose(ps[:, BANK_T, 0:B * N // P], mask_f, ident[0:B * N // P, 0:B * N // P]).then_inc(s_maskT, 1)
            pe.wait_ge(s_cond, 16 * (B + 2))
            for f in range(KC):
                for k in range(KC):
                    last = pe.matmul(ps[:, BANK_FEAT, f * B:(f + 1) * B], ada1_raw[:, k, f * P:(f + 1) * P], condT[:, k, :],
                                     start=k == 0, stop=k == KC - 1)
            last.then_inc(s_ada_mm, 1)

            def modulation(layer):
                pe.wait_ge(s_silu, 3)
                pe.wait_ge(s_ada_raw[layer], 16)
                for n in range(3):
                    for k in range(KC):
                        last = pe.matmul(ps[0:B, ADA_BANK[layer] + n, :], (silu0, silu1)[layer][:, k, :],
                                         ada_raw[:, k, n * CH:(n + 1) * CH], start=k == 0, stop=k == KC - 1)
                last.then_inc(s_ada_mm, 1)

            pe.wait_ge(s_dset, 4)
            pe.wait_ge(s_const, 5)
            pe.wait_ge(s_qkv_lo, 1)

            def body(b, seen):
                def transpose_pair(n, tiles):
                    for t in range(2):
                        for k in range(KC):
                            last = pe.transpose(ps[:, t_bank(n), (2 * k + t) * P:(2 * k + t + 1) * P],
                                                tiles[t][:, k * P:(k + 1) * P], ident[:, :])
                    last.then_inc(s_t_mm, 1)

                def transposes(step, src):
                    for pair in range(2):
                        n = T_AT[step] + pair
                        if t_before(n) >= 0:
                            pe.wait_ge(s_t_lo, b * T_N + t_before(n) + 1)
                        transpose_pair(n, [src[:, 2 * pair + t, :] for t in range(2)])


                def run(p, s, seen):
                    bank_t = None

                    def bank_evacuated(m):
                        if m >= 2:
                            kind, n = p.projected()[m - 2]
                            if kind == "k":
                                pe.wait_ge(s.k_lo, seen * p.k_tiles + n + 1)
                            else:
                                pe.wait_ge(s_q_lo, b * Q_N + n + 1)

                    def take_bank_t(sem_, value):
                        nonlocal bank_t
                        if bank_t is not None:
                            pe.wait_ge(*bank_t)
                        bank_t = (sem_, value)

                    kav = ka[:, :].rearrange("r (h n) -> r h n", h=p.heads)
                    for step in p.order():
                        if step[0] == "k":
                            n = step[1]
                            fc, blk = divmod(n, p.blocks)
                            m = p.projected().index(step)
                            bank_evacuated(m)
                            if n == 0:
                                pe.wait_ge(s_t_lo, b * T_N + T_AT["x", 1] + 2)
                            fs = slice(C + fc * P, C + (fc + 1) * P)
                            product(ps[:, BANK_FEAT + m % 2, 0:p.block],
                                    [[weights["qkv"][part][:, k, fs] for k in range(KC)] for part in range(2)],
                                    [x_tile(None, part, N - p.keys + blk * p.block, p.block) for part in range(2)])\
                                .then_inc(s.k_mm, 1)
                        elif step[0] == "x":
                            c = step[1]
                            pe.wait_ge(s_x[c], b * 16 + 16)
                            transposes(("x", c), x_tok[:, c * T:(c + 1) * T, :])
                        elif step[0] == "q":
                            n = step[1]
                            m = p.projected().index(step)
                            c, fc = divmod(n, KC)
                            bank_evacuated(m)
                            if n == 0:
                                pe.wait_ge(s_t_lo, b * T_N + T_AT["x", 0] + 2)
                            fs = slice(fc * P, (fc + 1) * P)
                            product(ps[:, BANK_FEAT + m % 2, :],
                                    [[weights["qkv"][part][:, k, fs] for k in range(KC)] for part in range(2)],
                                    [x_tile(None, part, c * CH, CH) for part in range(2)]).then_inc(s_q_mm, 1)
                        elif step[0] == "ada":
                            with pe.If(b == 0):
                                pe.wait_ge(s_q_lo, Q_N)
                                pe.wait_ge(s.v, 2 * p.kt)
                                modulation(step[1])
                        elif step[0] == "rows":
                            pe.wait_ge(s_ada_row, 1 + 5 * step[1])
                            pe.wait_ge(s_ones, 16)
                        elif step[0] == "upb":
                            with pe.If(b == 0):
                                pe.wait_ge(s_cols, 16 * KC * B)
                                pe.wait_ge(s_up_raw, 32)
                                up = [(up_raw[:, 0:2 * C].rearrange("p (k n) -> p k n", k=KC), 0, f) for f in range(C // P)] + \
                                     [(up_raw[:, 2 * C:6 * C].rearrange("p (k n) -> p k n", k=KC), 2, f) for f in range(FF1 // P)]
                                for i, (w, shift, f) in enumerate(up):
                                    for k in range(KC):
                                        last = pe.matmul(ps[:, BANK_FEAT, i * B:(i + 1) * B], w[:, k, f * P:(f + 1) * P],
                                                         cols[:, k, shift, :], start=k == 0, stop=k == KC - 1)
                                last.then_inc(s_upb, 1)
                        elif step[0] == "v":
                            n = step[1]
                            if n >= 4:
                                pe.wait_ge(s.v, seen * (2 * p.kt) + 2 * (n - 3))
                            product(ps[:, BANK_TOK + n % 4, 0:C],
                                    [x_tile(None, part, N - p.keys + n * P, P) for part in range(2)],
                                    [[weights["qkv"][part][:, k, 2 * C:3 * C] for k in range(KC)] for part in range(2)])\
                                .then_inc(s.v_mm, 1)
                        elif step[0] == "s1":
                            _, u, i = step
                            n, slot = u * p.n1 + i, u % QSLOTS
                            if i == 0:
                                if u == 0:
                                    pe.wait_ge(s.v, seen * (2 * p.kt) + 2 * p.kt)
                                if u == 0 or p is FULL:
                                    pe.wait_ge(s.ka, seen * (64 * (UNITS if p is FULL else 1)) + 64 * (u + 1))
                                pe.wait_ge(s.qa[slot], seen * (48 * slot_total(u)) + 48 * slot_uses(u))
                            if n >= 2:
                                pe.wait_ge(s.max, seen * (UNITS * p.n1) + n - 1)
                            bank = BANK_TOK + 2 + n % 2
                            if p is FAST:
                                h, tp = divmod(i, T // 2)
                                for t in range(2):
                                    q0 = (2 * tp + t) * P
                                    last = pe.matmul(ps[:, bank, t * p.keys:(t + 1) * p.keys], qa[0:ROWS_S1, slot, h, q0:q0 + P],
                                                     kav[0:ROWS_S1, (u % NG) * HG + h, :], start=True, stop=True)
                            else:
                                h, t, half = i // (2 * T), i // 2 % T, i % 2
                                last = pe.matmul(ps[:, bank, :], qa[0:ROWS_S1, slot, h, t * P:(t + 1) * P],
                                                 kav[0:ROWS_S1, h, half * CH:(half + 1) * CH], start=True, stop=True)
                            last.then_inc(s.s1, 1)
                        elif step[0] == "mT":
                            u = step[1]
                            take_bank_t(s.mT_sb, seen * UNITS + u + 1)
                            pe.wait_ge(s.neg, seen * (2 * UNITS) + 2 * (u + 1))
                            pe.transpose(ps[0:2 * HG * T, BANK_T, 0:P], mhl[:, u % 2, :].bitcast(F32), ident[:, :]).then_inc(s.mT, 1)
                        elif step[0] == "s2":
                            _, u, kt, hp = step
                            n, slot = u * p.n2 + 2 * kt + hp, u % QSLOTS
                            if kt == 0 and hp == 0:
                                pe.wait_ge(s.m[slot], seen * (32 * slot_total(u)) + 32 * slot_uses(u))
                            if n >= 2:
                                pe.wait_ge(s.exp, seen * (UNITS * p.n2) + n - 1)
                            for h in (2 * hp, 2 * hp + 1):
                                head = (u % NG) * HG + h if p.heads == H else h
                                last = pe.matmul(ps[:, h, :], kav[0:ROWS_S2, head, kt * P:(kt + 1) * P], qa[0:ROWS_S2, slot, h, :],
                                                 start=True, stop=True)
                            last.then_inc(s.s2, 1)
                        elif step[0] == "pv":
                            _, u, kt = step
                            pe.wait_ge(s.exp, seen * (UNITS * p.n2) + u * p.n2 + 2 * (kt + 1))
                            if kt == 0 and u >= 1:
                                pe.wait_ge(s.o_sb, seen * UNITS + u)
                            for h in range(HG):
                                last = pe.matmul(ps[32 * h:32 * h + VW, BANK_PV, :], v_sb[:, kt, (u % NG) * HG + h, :],
                                                 probs[:, kt % 2, h, :], start=kt == 0, stop=kt == p.kt - 1)
                            last.then_inc(s.pv, 1)
                        elif step[0] == "oT":
                            u = step[1]
                            take_bank_t(s.o, seen * UNITS + u + 1)
                            pe.wait_ge(s.o_sb, seen * UNITS + u + 1)
                            for t in range(T):
                                last = pe.transpose(ps[:, BANK_T, t * P:(t + 1) * P], o_sb[:, u % 2, t * P:(t + 1) * P], ident[:, :])
                            last.then_inc(s.oT, 1)
                        elif step[0] == "attnT":
                            c = step[1]
                            pe.wait_ge(s.o, seen * UNITS + (c + 1) * NG)
                            for pair in range(2):
                                n = T_AT["o", c] + pair
                                take_bank_t(s_t_lo, b * T_N + n + 1)
                                transpose_pair(n, [o_tok[:, 2 * pair + t, :] for t in range(2)])

                by_path(pe, b, seen, run)

                def tok_tile(n):
                    return ps[:, BANK_TOK + n % 4, 0:C]

                def take_tok(n):
                    if n >= 4:
                        pe.wait_ge(s_tok_free, b * (TOK_N // 2) + (n - 4) // 2 + 1)

                up_w = {"fc": "fc1", "ssm": "ssm1", "ff": "ff1"}
                down_w = {"fc": "fc2", "ssm": "ssm2", "ff": "ff2"}

                def up(step, j, slot):
                    n = H_AT[step] + j
                    if n >= 2:
                        pe.wait_ge(s_gelu, b * H_N + n - 1)
                    w = weights[up_w[step[0]]]
                    product(ps[:, BANK_FEAT + n % 2, :],
                            [[w[part][:, k, j * P:(j + 1) * P] for k in range(KC)] for part in range(2)],
                            [[actT[slot][part][:, k, :] for k in range(KC)] for part in range(2)]).then_inc(s_up_mm, 1)

                def down(step, j):
                    n = H_AT[step] + j
                    w = weights[down_w[step[0]]]
                    pe.wait_ge(s_h_lo, b * H_N + n + 1)
                    for t in range(T):
                        tok = TOK_AT[step] + t
                        if j == 0:
                            take_tok(tok)
                        last = product(tok_tile(tok),
                                       [[hid[:, n % HSLOTS, part, t * P:(t + 1) * P]] for part in range(2)],
                                       [[w[part][:, j, :]] for part in range(2)],
                                       start=j == 0, stop=j == HIDDEN[step[0]] - 1)
                        if j == HIDDEN[step[0]] - 1:
                            last.then_inc(s_tok_mm, 1)
                    pe.nop().then_inc(s_h_used, 1) if j == HIDDEN[step[0]] - 1 else last.then_inc(s_h_used, 1)

                pe.wait_ge(s_upb, 2)
                pe.wait_ge(s_split, SPLITS)
                for step in MLP_ORDER:
                    kind, c = step
                    if kind == "proj":
                        pe.wait_ge(s_t_lo, b * T_N + T_AT["o", c] + 2)
                        for t in range(T):
                            n = TOK_AT[step] + t
                            take_tok(n)
                            product(tok_tile(n),
                                    [[actT["AB"[c]][part][:, k, t * P:(t + 1) * P] for k in range(KC)] for part in range(2)],
                                    [[weights["proj"][part][:, k, :] for k in range(KC)] for part in range(2)])\
                                .then_inc(s_tok_mm, 1)
                    elif kind == "T1":
                        for pair in range(2):
                            n = T_AT[step] + pair
                            if t_before(n) >= 0:
                                pe.wait_ge(s_t_lo, b * T_N + t_before(n) + 1)
                            pe.wait_ge(s_norm, b * (2 * LN_N) + 2 * (LN_AT["proj", c] + pair + 1))
                            transpose_pair(n, [x_tok[:, c * T + 2 * pair + t, :] for t in range(2)])
                    elif kind in ("T2", "T3"):
                        for pair in range(2):
                            n = T_AT[step] + pair
                            if t_before(n) >= 0:
                                pe.wait_ge(s_t_lo, b * T_N + t_before(n) + 1)
                            pe.wait_ge(s_norm, b * (2 * LN_N) + 2 * (LN_AT[step] + pair + 1))
                            transpose_pair(n, [a_tok[c][:, 2 * pair + t, :] for t in range(2)])
                    else:
                        slot = "CA"[c]
                        last_t = {"fc": "T1", "ssm": "T2", "ff": "T3"}[kind]
                        pe.wait_ge(s_t_lo, b * T_N + T_AT[last_t, c] + 2)
                        if kind != "fc" and c == 0:
                            pe.wait_ge(s_wmod, b * 4 + 4)
                        total = HIDDEN[kind]
                        for j in range(total + 2):
                            if j < total:
                                up(step, j, slot)
                            if j >= 2:
                                down(step, j - 2)

            batches(pe, body)


_INS = ["x", "cond_1024", "mask_BxS_bk0"] + \
    ["L0_cond_" + n for n in ("qkv_w", "proj_w", "proj_b", "fc1_w", "fc1_b", "fc2_w", "fc2_b", "ada1_w", "ada1_b", "ada2_w", "ada2_b")] + \
    ["L1_cond_" + n for n in ("ada_w", "ada_b", "ssm_w1", "ssm_b1", "ssm_w2", "ssm_b2", "ff_w1", "ff_b1", "ff_w2", "ff_b2")]


def kernel(**inputs):
    import numpy as np
    import concourse.bacc as bacc
    from concourse.bass_utils import run_bass_kernel_spmd

    nc = bacc.Bacc("TRN2", target_bir_lowering=False, num_devices=1, dynamic_dma_scratch_size=8192)
    arrays, args = {}, []
    for name in _INS:
        a = np.ascontiguousarray(inputs[name])
        arrays[f"in_{name}"] = a
        args.append(nc.dram_tensor(f"in_{name}", a.shape, mybir.dt.from_np(a.dtype), kind="ExternalInput").ap())
    args.append(nc.dram_tensor("out_0", (B, N, C), F32, kind="ExternalOutput").ap())
    build(nc, *args)
    r = run_bass_kernel_spmd(nc, [arrays], core_ids=[0])
    return r.results[0]["out_0"]
```
